# Optimizing a Trainium2 kernel written in Bass

```python
import numpy as np
import jax
import jax.numpy as jnp

def _softmax(x, axis=-1):
    return jax.nn.softmax(x, axis=axis)

def _gelu(x):
    return jax.nn.gelu(x, approximate=True)

def _silu(x):
    return jax.nn.silu(x)

def _sigmoid(x):
    return jax.nn.sigmoid(x)

def _layernorm(x, axis=-1, eps=1e-05):
    m = jnp.mean(x, axis=axis, keepdims=True)
    v = jnp.var(x, axis=axis, keepdims=True)
    return (x - m) / jnp.sqrt(v + eps)

def _scatter_add(tgt, idx, src, axis=0):
    return tgt.at[idx].add(src)

def _segment_sum(src, seg, n):
    return jax.ops.segment_sum(src, seg, n)
kernel_name = 'mk_adj_resnorm_d2_adj_r2_957858'

def setup_inputs(seed: int=0):
    np.random.seed(seed)
    _w = jnp.asarray

    def _rec_inputs():
        import jax
        import jax.numpy as jnp
        _gk = jax.random.key(seed)
        x = -0.000125 + 0.9999 * jax.random.normal(jax.random.fold_in(_gk, 1), (16, 512, 512), jnp.float32)
        _a = jax.random.bernoulli(jax.random.fold_in(_gk, 2), 0.00390625, (16, 512, 512))
        _a = jnp.logical_or(_a, jnp.swapaxes(_a, -1, -2))
        _a = jnp.logical_or(_a, jnp.eye(512, dtype=bool))
        _af = _a.astype(jnp.float32)
        _af = _af * jax.random.uniform(jax.random.fold_in(_gk, 3), (16, 512, 512), jnp.float32, 0.05, 0.999994)
        adj = _af
        return (x, adj)
    x, adj = _rec_inputs()

    def _L0_gnn_setup():
        import jax, jax.numpy as jnp
        import numpy as np
        B, N, H, E = (64, 256, 512, 4)
        BN_EPS = 1e-05
        key = jax.random.key(seed)
        ks = jax.random.split(key, 6)
        x = jax.random.normal(ks[0], (B, N, H), dtype=jnp.float32)
        adj = jax.random.uniform(ks[1], (B, N, N), dtype=jnp.float32)
        stdv = 1.0 / np.sqrt(H)
        expert_w = jax.random.uniform(ks[2], (E, H, H), minval=-stdv, maxval=stdv, dtype=jnp.float32)
        r_std = 1.0 / np.sqrt(H)
        router_w = jax.random.uniform(ks[3], (H, E), minval=-r_std, maxval=r_std, dtype=jnp.float32)
        router_b = jax.random.uniform(ks[4], (E,), minval=-r_std, maxval=r_std, dtype=jnp.float32)
        bn_gamma = jnp.ones((E, H), dtype=jnp.float32)
        bn_beta = jnp.zeros((E, H), dtype=jnp.float32)
        return {'x': x, 'adj': adj, 'router_w': router_w, 'router_b': router_b, 'expert_w': expert_w, 'bn_gamma': bn_gamma, 'bn_beta': bn_beta}
    _L0_gnn_all = _L0_gnn_setup()
    _L0_gnn_in = {k: v for k, v in _L0_gnn_all.items() if k in ('router_w', 'router_b', 'expert_w', 'bn_gamma', 'bn_beta')}
    del _L0_gnn_all

    def _L1_gnn_setup():
        import jax, jax.numpy as jnp
        import numpy as np
        NUM_HEADS = 16
        key = jax.random.key(seed)
        ks = jax.random.split(key, 7)
        B, N, D = (16, 256, 512)
        return {'x': jax.random.normal(ks[0], (B, N, D), dtype=jnp.float32), 'spatial_encoding': jax.random.normal(ks[1], (B, N, N), dtype=jnp.float32), 'edge_encoding': jax.random.normal(ks[2], (B, N, N), dtype=jnp.float32), 'Wq': jax.random.normal(ks[3], (D, D), dtype=jnp.float32) * D ** (-0.5), 'Wk': jax.random.normal(ks[4], (D, D), dtype=jnp.float32) * D ** (-0.5), 'Wv': jax.random.normal(ks[5], (D, D), dtype=jnp.float32) * D ** (-0.5), 'Wo': jax.random.normal(ks[6], (D, D), dtype=jnp.float32) * D ** (-0.5)}
    _L1_gnn_all = _L1_gnn_setup()
    _L1_gnn_in = {k: v for k, v in _L1_gnn_all.items() if k in ('Wq', 'Wk', 'Wv', 'Wo')}
    del _L1_gnn_all
    return {'x': x, 'adj': adj, 'L0_gnn_router_w': _L0_gnn_in['router_w'], 'L0_gnn_router_b': _L0_gnn_in['router_b'], 'L0_gnn_expert_w': _L0_gnn_in['expert_w'], 'L0_gnn_bn_gamma': _L0_gnn_in['bn_gamma'], 'L0_gnn_bn_beta': _L0_gnn_in['bn_beta'], 'L1_gnn_Wq': _L1_gnn_in['Wq'], 'L1_gnn_Wk': _L1_gnn_in['Wk'], 'L1_gnn_Wv': _L1_gnn_in['Wv'], 'L1_gnn_Wo': _L1_gnn_in['Wo']}

def reference(x, adj, L0_gnn_router_w, L0_gnn_router_b, L0_gnn_expert_w, L0_gnn_bn_gamma, L0_gnn_bn_beta, L1_gnn_Wq, L1_gnn_Wk, L1_gnn_Wv, L1_gnn_Wo):
    import jax
    import jax.numpy as jnp

    def _L0_gnn_ref(x, adj, router_w, router_b, expert_w, bn_gamma, bn_beta):
        import jax, jax.numpy as jnp
        import numpy as np
        B, N, H, E = (64, 256, 512, 4)
        BN_EPS = 1e-05
        scores = x.mean(axis=1) @ router_w + router_b
        top1 = jnp.argmax(scores, axis=-1)
        n_exp = expert_w.shape[0]
        W = expert_w[top1]
        support = jnp.einsum('bnh,bhk->bnk', x, W)
        out = jnp.einsum('bnm,bmk->bnk', adj, support)
        s = jax.ops.segment_sum(out.sum(axis=1), top1, num_segments=n_exp)
        ss = jax.ops.segment_sum((out * out).sum(axis=1), top1, num_segments=n_exp)
        cnt = jax.ops.segment_sum(jnp.ones_like(top1, dtype=out.dtype), top1, num_segments=n_exp) * out.shape[1]
        cnt = jnp.maximum(cnt, 1.0)[:, None]
        mean = s / cnt
        var = ss / cnt - mean * mean
        m = mean[top1][:, None, :]
        inv = jax.lax.rsqrt(var[top1][:, None, :] + BN_EPS)
        y = (out - m) * inv * bn_gamma[top1][:, None, :] + bn_beta[top1][:, None, :]
        return jax.nn.relu(y)

    def _L1_gnn_ref(x, spatial_encoding, edge_encoding, Wq, Wk, Wv, Wo):
        import jax, jax.numpy as jnp
        import numpy as np
        NUM_HEADS = 16
        B, N, D = x.shape
        H = NUM_HEADS
        hd = D // H
        scale = D ** (-0.5)

        def split_heads(t):
            return t.reshape(B, N, H, hd).transpose(0, 2, 1, 3)
        q = split_heads(x @ Wq.T)
        k = split_heads(x @ Wk.T)
        v = split_heads(x @ Wv.T)
        bias = (spatial_encoding + edge_encoding)[:, None]
        a = jnp.einsum('bhnd,bhmd->bhnm', q, k) * scale + bias
        row_nonzero = jnp.any(a != 0, axis=-1, keepdims=True)
        a = jnp.where(row_nonzero, a, -jnp.inf)
        p = jax.nn.softmax(a, axis=-1)
        p = jnp.where(jnp.isnan(p), 0.0, p)
        o = jnp.einsum('bhnm,bhmd->bhnd', p, v)
        o = o.transpose(0, 2, 1, 3).reshape(B, N, D)
        return o @ Wo.T
    x = _layernorm(x + _L0_gnn_ref(x, adj, L0_gnn_router_w, L0_gnn_router_b, L0_gnn_expert_w, L0_gnn_bn_gamma, L0_gnn_bn_beta), axis=-1)
    x = _layernorm(x + _L1_gnn_ref(x, adj, adj, L1_gnn_Wq, L1_gnn_Wk, L1_gnn_Wv, L1_gnn_Wo), axis=-1)
    return x

_drawn_inputs = setup_inputs


def setup_inputs(seed=0):
    import zlib

    import numpy as np

    out = dict(_drawn_inputs(seed))
    spreads = {'L0_gnn_bn_gamma': (1.0, 0.2), 'L0_gnn_bn_beta': (0.0, 0.1)}
    factors = {'L1_gnn_Wq': 3.478, 'L1_gnn_Wk': 3.484}
    for name, (base, spread) in spreads.items():
        noise = np.random.default_rng([zlib.crc32(name.encode()), seed]).standard_normal(out[name].shape)
        drawn = base * np.exp(spread * noise) if base else spread * noise
        out[name] = jnp.asarray(drawn.astype(out[name].dtype))
    for name, factor in factors.items():
        out[name] = (out[name] * factor).astype(out[name].dtype)
    return out
```

```python
from contextlib import ExitStack

import concourse.bass as bass
from concourse import mybir

P = 128
ALU = mybir.AluOpType
ACT = mybir.ActivationFunctionType
AX = mybir.AxisListType
F32 = mybir.dt.float32
F32R = mybir.dt.float32r
U32 = mybir.dt.uint32

B, N, H = 16, 512, 512
NT = N // P
E = 4
HEADS, HD = 16, 32
G = HEADS // NT
J = 4
STEPS = G * NT
EPS = 1e-5
LOWEST = -3.0e38
QSCALE = float(H) ** -0.5 / 2.0
PARTS = ((0, 0), (0, 1), (1, 0))

SLOTS = ([("o", i, -1) for i in range(4)]
         + [("k", 2, 0), ("q", 2, 0), ("k", 3, 0), ("q", 3, 0)]
         + [("v", i, 1) for i in range(4)]
         + [("k", 0, 1), ("q", 0, 1), ("k", 1, 1), ("q", 1, 1)])
XT_STEP = 8
Y_STEP = 4


def need(eng, sem, count):
    if not isinstance(count, int) or count > 0:
        eng.wait_ge(sem, count)


def f32(ap):
    return ap.bitcast(F32)


def gnn_program(nc, x, adj, router_w, router_b, expert_w, bn_gamma, bn_beta, Wq, Wk, Wv, Wo, out):
    outT_dram = nc.dram_tensor("outT_spill", [B, H, N], F32).ap()
    x1_dram = nc.dram_tensor("x1_spill", [B, N, H], F32).ap()

    def rows(dram, b):
        return dram[bass.ds(b, 1)].rearrange("o (t p) n -> p (o t) n", p=P)

    def row_tile(dram, b, t):
        return dram[bass.ds(b, 1), t * P:(t + 1) * P, :].rearrange("o p n -> p (o n)")

    with ExitStack() as ctx:
        sems = {}

        def sem(name):
            sems[name] = ctx.enter_context(nc.semaphore(name))
            return sems[name]

        def sb(stack, name, shape, dt=F32):
            return stack.enter_context(nc.sbuf_tensor(name, shape, dt))

        bank = [ctx.enter_context(nc.psum_tensor(f"bank{i}", [P, 512], F32)) for i in range(8)]

        ident = sb(ctx, "ident", [P, P])
        bn_scale = sb(ctx, "bn_scale", [P, B, NT])
        bn_bias = sb(ctx, "bn_bias", [P, B, NT])
        minus_half = sb(ctx, "minus_half", [P, 16])

        with ExitStack() as l0:
            w_exp = [sb(l0, f"w_exp{p}", [P, E, NT, H], F32R) for p in range(2)]
            raw = [sb(l0, f"w_raw{i}", [P, NT, H]) for i in range(4)]
            w_sel = [sb(l0, f"w_sel{p}", [P, NT, H], F32R) for p in range(2)]
            x_raw = sb(l0, "x_raw", [P, NT, H])
            adj_raw = sb(l0, "adj_raw", [P, NT, N])
            x_part = [sb(l0, f"x_part{p}", [P, NT, H], F32R) for p in range(2)]
            adjT = [sb(l0, f"adjT{p}", [P, NT, N], F32R) for p in range(2)]
            zT = [sb(l0, f"zT{p}", [P, NT, N], F32R) for p in range(2)]
            outT = sb(l0, "outT", [P, NT, N])
            x_sum = sb(l0, "x_sum", [P, H])
            inv_n = sb(l0, "inv_n", [P, 1])
            x_mean = sb(l0, "x_mean", [P, NT])
            rw = sb(l0, "rw", [P, NT, E])
            rb = sb(l0, "rb", [1, E])
            score8 = sb(l0, "score8", [1, 8])
            best8 = sb(l0, "best8", [1, 8])
            index8 = sb(l0, "index8", [1, 8], U32)
            indexf = sb(l0, "indexf", [1, 8])
            expert_no = sb(l0, "expert_no", [1, E])
            onehot_row = sb(l0, "onehot_row", [1, B, E])
            ones_row = sb(l0, "ones_row", [1, P])
            st_bn = sb(l0, "st_bn", [P, NT, 6])
            mv_now = sb(l0, "mv_now", [P, NT, 2])
            mv = sb(l0, "mv", [P, B, NT * 2])
            gb_rows = sb(l0, "gb_rows", [2 * E * NT, P])
            gam_bet = sb(l0, "gam_bet", [P, 2, E, NT])
            onehot = sb(l0, "onehot", [P, B, E])
            ex2 = sb(l0, "ex2", [P, B, NT])
            prod = sb(l0, "prod", [P, E * NT * B])
            sum1 = sb(l0, "sum1", [P, E, NT])
            sum2 = sb(l0, "sum2", [P, E, NT])
            inv_cnt = sb(l0, "inv_cnt", [P, E])
            scale_e = sb(l0, "scale_e", [P, E, NT])
            bias_e = sb(l0, "bias_e", [P, E, NT])

        with ExitStack() as l1:
            wT = {m: [sb(l1, f"w{m}T{p}", [P, NT, H], F32R) for p in range(2)] for m in "kqvo"}
            kp = sb(l1, "kp", [P, 2, J, N], F32R)
            qp = sb(l1, "qp", [P, 2, J, N], F32R)
            xT = [sb(l1, f"xT{p}", [P, NT, N], F32R) for p in range(2)]
            oT = [sb(l1, f"oT{p}", [P, NT, N], F32R) for p in range(2)]
            v = sb(l1, "v", [P, 2, NT, H])
            prob = sb(l1, "prob", [P, 2, J, N])
            probT = sb(l1, "probT", [P, J, NT, P])
            adj_sb = sb(l1, "adj_sb", [P, NT, N])
            yT = sb(l1, "yT", [P, NT, N])
            z = sb(l1, "z", [P, NT, H])
            stage = {m: [sb(l1, f"stage_{m}{p}", [P, N], F32R) for p in range(2)] for m in "kq"}
            recip = sb(l1, "recip", [P, N])
            recip_wide = sb(l1, "recip_wide", [P, NT * J, HD])
            row_max = sb(l1, "row_max", [P, 2, NT * J])
            row_sum = sb(l1, "row_sum", [P, 2, NT * J])
            neg_max = sb(l1, "neg_max", [P, 2, J])
            is_512 = sb(l1, "is_512", [P, NT * J])
            live = sb(l1, "live", [P, NT * J])
            inv_sum = sb(l1, "inv_sum", [P, NT * J])
            st_ln = sb(l1, "st_ln", [P, 2, 2, 6])
            mv_ln = sb(l1, "mv_ln", [P, 2, 2, 2])
            veps = sb(l1, "veps", [P, 2, 2, 1])
            rstd = sb(l1, "rstd", [P, 2, 2, 1])

        consts_made = sem("consts_made")
        ident_zero = sem("ident_zero")
        small_in = sem("small_in")
        experts_in = sem("experts_in")
        experts_hi = sem("experts_hi")
        experts_lo = sem("experts_lo")
        raw_in = [sem(f"raw_in{i}") for i in range(4)]
        adj_in = sem("adj_in")
        x_in = sem("x_in")
        adjT_ps = sem("adjT_ps")
        adjT_hi = sem("adjT_hi")
        adjT_lo = sem("adjT_lo")
        x_hi = sem("x_hi")
        x_lo = sem("x_lo")
        x_added = sem("x_added")
        mean_ps = sem("mean_ps")
        mean_sb = sem("mean_sb")
        score_ps = sem("score_ps")
        route = sem("route")
        sel_hi = sem("sel_hi")
        sel_lo = sem("sel_lo")
        z_ps = sem("z_ps")
        z_hi = sem("z_hi")
        z_lo = sem("z_lo")
        outT_ps = sem("outT_ps")
        outT_sb = sem("outT_sb")
        outT_st = sem("outT_st")
        outT_mv = sem("outT_mv")
        outT_kept = sem("outT_kept")
        outT_spilled = sem("outT_spilled")
        onehot_ps = sem("onehot_ps")
        bn_chain = sem("bn_chain")
        bn_pow = sem("bn_pow")
        bn_ready = sem("bn_ready")

        w_ps = sem("w_ps")
        w_hi = sem("w_hi")
        w_lo = sem("w_lo")
        adj1_in = [sem(f"adj1_in{t}") for t in range(NT)]
        yT_in = sem("yT_in")
        x1_x_in = [sem(f"x1_x_in{t}") for t in range(NT)]
        yT_relu = sem("yT_relu")
        y_ps = sem("y_ps")
        y_sum = sem("y_sum")
        y_st = sem("y_st")
        y_mv = sem("y_mv")
        y_eps = sem("y_eps")
        y_rstd = sem("y_rstd")
        x1_done = sem("x1_done")
        x1_spilled = sem("x1_spilled")
        x1_back = sem("x1_back")
        xT_ps = sem("xT_ps")
        xT_hi = sem("xT_hi")
        xT_lo = sem("xT_lo")
        dense_ps = {m: sem(f"dense_ps_{m}") for m in "kqvo"}
        stage_hi = {m: sem(f"stage_hi_{m}") for m in "kq"}
        stage_lo = {m: sem(f"stage_lo_{m}") for m in "kq"}
        packed = {m: sem(f"packed_{m}") for m in "kq"}
        v_done = sem("v_done")
        s_ps = sem("s_ps")
        s_max = sem("s_max")
        neg_done = sem("neg_done")
        exp_done = sem("exp_done")
        p_ps = sem("p_ps")
        pT_act = sem("pT_act")
        pT_dve = sem("pT_dve")
        pv_ps = sem("pv_ps")
        live_chain = sem("live_chain")
        inv_half = sem("inv_half")
        inv_done = sem("inv_done")
        wide_done = sem("wide_done")
        r_ps = sem("r_ps")
        r_sb = sem("r_sb")
        o_norm = sem("o_norm")
        oT_hi = sem("oT_hi")
        oT_lo = sem("oT_lo")
        f_sum = sem("f_sum")
        f_st = sem("f_st")
        f_mv = sem("f_mv")
        f_eps = sem("f_eps")
        f_rstd = sem("f_rstd")
        f_done = sem("f_done")
        out_stored = [sem(f"out_stored{t}") for t in range(NT)]

        freed = {"k": stage_lo["k"], "q": stage_lo["q"], "v": v_done, "o": f_sum}

        adjT_bank, dense0_bank, mean_bank, score_bank = bank[0:4], bank[4:6], bank[6], bank[7]
        s_bank, t_bank, pv_bank, dense_bank = bank[0:4], bank[4:6], bank[6], bank[7]

        def wait_apart(eng, sem, count):
            if isinstance(count, int):
                need(eng, sem, count)
            else:
                count = eng.to_reg(count)
                eng.wait_ge(ident_zero, 1)
                eng.wait_ge(sem, count)

        def layer0_over(eng):
            eng.wait_ge(outT_ps, NT * B)
            eng.wait_ge(outT_sb, NT * B)
            eng.wait_ge(outT_kept, B)
            eng.wait_ge(outT_spilled, 16 * B)

        def iterations(eng, body):
            body(0, 0, True, False)
            with eng.Fori(0, B // 2 - 1) as i:
                body(i * 2 + 1, 1, False, False)
                body(i * 2 + 2, 0, False, False)
            body(B - 1, 1, False, True)

        def is_live(slot, first, last):
            rel = SLOTS[slot][2]
            return not (rel < 0 and first) and not (rel > 0 and last)

        block = ctx.enter_context(nc.Block())

        @block.sync
        def _(sp):
            def load0(b):
                wait_apart(sp, adjT_ps, NT * b)
                sp.dma_start(adj_raw[:, :, :], rows(adj, b)).then_inc(adj_in, 16)
                wait_apart(sp, x_lo, b)
                wait_apart(sp, x_hi, b)
                wait_apart(sp, x_added, 3 * b)
                sp.dma_start(x_raw[:, :, :], rows(x, b)).then_inc(x_in, 16)

            def spill_outT(b):
                wait_apart(sp, outT_sb, NT * b + NT)
                sp.dma_start(rows(outT_dram, b), outT[:, :, :]).then_inc(outT_spilled, 16)

            load0(0)
            for e in range(E):
                sp.dma_start(raw[e][:, :, :], expert_w[e].rearrange("(t p) n -> p t n", p=P)).then_inc(experts_in, 16)
            sp.dma_start(rw[:, :, :], router_w.rearrange("(t p) e -> p t e", p=P)).then_inc(small_in, 16)
            sp.dma_start(rb[:, :], router_b.rearrange("(o e) -> o e", o=1)).then_inc(small_in, 16)
            for n, w in enumerate((bn_gamma, bn_beta)):
                sp.dma_start(gb_rows[n * E * NT:(n + 1) * E * NT, :],
                             w.rearrange("e (t p) -> (e t) p", p=P)).then_inc(small_in, 16)
            load0(1)
            spill_outT(0)
            with sp.Fori(1, B - 1) as b:
                load0(b + 1)
                spill_outT(b)
            spill_outT(B - 1)

            def load_adj(b, t, reused):
                if reused:
                    wait_apart(sp, s_max, 64 * (b - 1) + J * (12 + t) + J)
                sp.dma_start(adj_sb[:, t, :], row_tile(adj, b, t)).then_inc(adj1_in[t], 16)

            def load_yT(b):
                wait_apart(sp, y_ps, NT * b)
                sp.dma_start(yT[:, :, :], rows(outT_dram, b)).then_inc(yT_in, 16)

            def pack(m, b, g):
                ring = g % 2
                wait_apart(sp, s_ps, 64 * b + 16 * (g - 1))
                wait_apart(sp, stage_lo[m], NT * b + g + 1)
                dst = kp if m == "k" else qp
                for part in range(4):
                    src = stage[m][(part % 2) if m == "k" else (part // 2)]
                    sp.dma_start(f32(dst[part * HD:(part + 1) * HD, ring, :, :]).rearrange("p j n -> p (j n)"),
                                 f32(src[:, :])).then_inc(packed[m], 16)

            def spill_x1(b):
                wait_apart(sp, x1_done, NT * b + NT)
                sp.dma_start(rows(x1_dram, b), z[:, :, :]).then_inc(x1_spilled, 16)

            def store_out(b, t):
                wait_apart(sp, f_done, NT * b + t + 1)
                sp.dma_start(row_tile(out, b, t), z[:, t, :]).then_inc(out_stored[t], 16)

            def load_x(b, t):
                sp.dma_start(z[:, t, :], row_tile(x, b, t)).then_inc(x1_x_in[t], 16)

            layer0_over(sp)
            load_yT(0)
            sp.wait_ge(bn_ready, 1)
            for t in range(NT):
                load_x(0, t)
            for t in range(NT):
                load_adj(0, t, False)
            spill_x1(0)
            for g in range(2):
                pack("k", 0, g)
                pack("q", 0, g)

            def batch(b, par, first, last):
                if not last:
                    load_yT(b + 1)
                for s in range(STEPS):
                    if 1 <= s <= 4 and not first:
                        store_out(b - 1, s - 1)
                    if first and s == 1:
                        wait_apart(sp, x1_spilled, 16)
                        wait_apart(sp, xT_ps, NT)
                    if 2 <= s <= 5 and not last:
                        if not first:
                            wait_apart(sp, out_stored[s - 2], 16 * b)
                        load_x(b + 1, s - 2)
                    if last and s == 5:
                        for t in range(NT):
                            wait_apart(sp, out_stored[t], 16 * b)
                    kind, i, rel = SLOTS[s]
                    if s >= 12 and not last:
                        load_adj(b + 1, s - 12, True)
                    if kind in "kq" and is_live(s, first, last):
                        pack(kind, b + rel, i)
                    if s == 8 and not last:
                        spill_x1(b + 1)
                    if s == 10:
                        if not last:
                            wait_apart(sp, x1_spilled, 16 * (b + 2))
                            wait_apart(sp, xT_ps, NT * (b + 2))
                        sp.dma_start(z[:, :, :], rows(x1_dram, b)).then_inc(x1_back, 16)

            iterations(sp, batch)
            for t in range(NT):
                store_out(B - 1, t)
            for t in range(NT):
                wait_apart(sp, out_stored[t], 16 * B)

        @block.gpsimd
        def _(pool):
            nc.gpsimd.memset(ident[:, :], 0.0).then_inc(ident_zero, 1)
            pool.wait_ge(ident_zero, 1)
            nc.gpsimd.affine_select(out=ident[:, :], in_=ident[:, :], compare_op=ALU.not_equal, fill=1.0,
                                    base=0, pattern=[[-1, P]], channel_multiplier=1).then_inc(consts_made, 1)
            nc.gpsimd.memset(minus_half[:, :], -0.5).then_inc(consts_made, 1)
            nc.gpsimd.memset(inv_n[:, :], 1.0 / N).then_inc(consts_made, 1)
            nc.gpsimd.memset(ones_row[:, :], 1.0).then_inc(consts_made, 1)
            nc.gpsimd.memset(score8[:, :], LOWEST).then_inc(consts_made, 1)
            for e in range(E):
                nc.gpsimd.memset(expert_no[:, e:e + 1], float(e)).then_inc(consts_made, 1)

            def split_x(b):
                pool.wait_ge(x_hi, b + 1)
                need(pool, z_ps, NT * b)
                for t in range(NT):
                    ins = nc.gpsimd.tensor_tensor(x_part[1][:, t, :], x_raw[:, t, :], f32(x_part[0][:, t, :]),
                                                  ALU.subtract)
                ins.then_inc(x_lo, 1)

            split_x(0)
            pool.wait_ge(experts_lo, E)
            for i, w in enumerate((Wk, Wq)):
                by_head = w.rearrange("(t j d) n -> j d t n", j=J, d=HD)
                for j in range(J):
                    pool.dma_start(raw[i][j:P - J + j + 1:J, :, :], by_head[j]).then_inc(raw_in[i], 16)
            for i, w in ((2, Wv), (3, Wo)):
                pool.dma_start(raw[i][:, :, :], w.rearrange("(t p) n -> p t n", p=P)).then_inc(raw_in[i], 16)
            with pool.Fori(0, B - 1) as b:
                split_x(b + 1)

            pool.wait_ge(bn_chain, BN_VAR)
            nc.gpsimd.tensor_tensor(sum2[:, :, :].rearrange("p e t -> p (e t)"),
                                    sum2[:, :, :].rearrange("p e t -> p (e t)"),
                                    minus_half[:, :], ALU.pow).then_inc(bn_pow, 1)

            def layer_norm_rstd(which, b, t, mv_sem, eps_sem, rstd_sem):
                wait_apart(pool, mv_sem, NT * b + t + 1)
                nc.gpsimd.tensor_scalar(veps[:, which, t % 2, :], mv_ln[:, which, t % 2, 1:2], EPS, None,
                                        ALU.add).then_inc(eps_sem, 1)
                pool.wait_ge(eps_sem, NT * b + t + 1)
                nc.gpsimd.tensor_tensor(rstd[:, which, t % 2, :], veps[:, which, t % 2, :],
                                        minus_half[:, 0:1], ALU.pow).then_inc(rstd_sem, 1)

            def softmax_weights(b, g):
                ring = g % 2
                n = 3 * (G * b + g)
                wait_apart(pool, exp_done, 64 * b + 16 * g + 16)
                nc.gpsimd.tensor_scalar(is_512[:, :], row_sum[:, ring, :], float(N), None,
                                        ALU.is_equal).then_inc(live_chain, 1)
                nc.gpsimd.tensor_scalar(live[:, :], row_max[:, ring, :], 0.0, None,
                                        ALU.is_equal).then_inc(live_chain, 1)
                pool.wait_ge(live_chain, n + 2)
                nc.gpsimd.tensor_tensor(live[:, :], live[:, :], is_512[:, :], ALU.mult).then_inc(live_chain, 1)
                wait_apart(pool, live_chain, n + 3)
                wait_apart(pool, inv_done, G * b + g + 1)
                wait_apart(pool, r_ps, G * b + g)
                nc.gpsimd.tensor_scalar(recip_wide[:, :, :],
                                        inv_sum[:, :].rearrange("p (a o) -> p a o", o=1).broadcast_to([P, NT * J, HD]),
                                        1.0, None, ALU.mult).then_inc(wide_done, 1)

            for t in range(NT):
                layer_norm_rstd(0, 0, t, y_mv, y_eps, y_rstd)

            def batch(b, par, first, last):
                for s in range(STEPS):
                    if s % NT == 3:
                        softmax_weights(b, s // NT)
                    if s < NT and not first:
                        layer_norm_rstd(1, b - 1, s, f_mv, f_eps, f_rstd)
                    if Y_STEP <= s < Y_STEP + NT and not last:
                        layer_norm_rstd(0, b + 1, s - Y_STEP, y_mv, y_eps, y_rstd)

            iterations(pool, batch)
            for t in range(NT):
                layer_norm_rstd(1, B - 1, t, f_mv, f_eps, f_rstd)

        @block.tensor
        def _(pe):
            mm = nc.tensor.matmul

            def transpose_adj(b):
                pe.wait_ge(adj_in, 16 * b + 16)
                need(pe, adjT_lo, NT * b)
                for mt in range(NT):
                    for nt in range(NT):
                        ins = nc.tensor.transpose(adjT_bank[mt][:, nt * P:(nt + 1) * P],
                                                  adj_raw[:, nt, mt * P:(mt + 1) * P], ident[:, :])
                    ins.then_inc(adjT_ps, 1)

            def z_tiles(b):
                pe.wait_ge(x_lo, b + 1)
                for i in range(NT):
                    if i < 2:
                        need(pe, outT_sb, NT * (b - 1) + 3 + i)
                    else:
                        pe.wait_ge(z_lo, NT * b + i - 1)
                    ps = dense0_bank[i % 2]
                    for mt in range(NT):
                        if i == 0:
                            pe.wait_ge(adjT_lo, NT * b + mt + 1)
                        for n, (a, c) in enumerate(PARTS):
                            ins = mm(ps[:, :], x_part[a][:, mt, i * P:(i + 1) * P], adjT[c][:, mt, :],
                                     start=(mt == 0 and n == 0), stop=(mt == NT - 1 and n == 2))
                    ins.then_inc(z_ps, 1)

            def out_tile(b, i):
                if i == 0:
                    pe.wait_ge(sel_lo, b + 1)
                if i < 2:
                    pe.wait_ge(z_lo, NT * b + 3 + i)
                else:
                    pe.wait_ge(outT_sb, NT * b + i - 1)
                if i == 0:
                    pe.wait_ge(z_lo, NT * b + NT)
                ps = dense0_bank[i % 2]
                for ht in range(NT):
                    for n, (a, c) in enumerate(PARTS):
                        ins = mm(ps[:, :], w_sel[a][:, ht, i * P:(i + 1) * P], zT[c][:, ht, :],
                                 start=(ht == 0 and n == 0), stop=(ht == NT - 1 and n == 2))
                ins.then_inc(outT_ps, 1)

            def x_mean_product(b):
                pe.wait_ge(x_added, 3 * b + 3)
                need(pe, mean_sb, b)
                for t in range(NT):
                    ins = mm(mean_bank[:, t:t + 1], x_sum[:, t * P:(t + 1) * P], inv_n[:, :], start=True, stop=True)
                ins.then_inc(mean_ps, 1)

            def score_product(b):
                pe.wait_ge(mean_sb, b + 1)
                need(pe, route, 5 * b)
                for t in range(NT):
                    ins = mm(score_bank[0:1, 0:E], x_mean[:, t:t + 1], rw[:, t, :], start=(t == 0), stop=(t == NT - 1))
                ins.then_inc(score_ps, 1)

            pe.wait_ge(consts_made, 5 + E)
            pe.wait_ge(small_in, 16 * 4)
            transpose_adj(0)
            x_mean_product(0)
            score_product(0)
            z_tiles(0)
            def batch0(b):
                transpose_adj(b + 1)
                out_tile(b, 0)
                out_tile(b, 1)
                x_mean_product(b + 1)
                out_tile(b, 2)
                score_product(b + 1)
                out_tile(b, 3)
                z_tiles(b + 1)

            batch0(0)
            with pe.Fori(1, B - 1) as b:
                batch0(b)
            for i in range(NT):
                out_tile(B - 1, i)

            pe.wait_ge(route, 5 * B)
            pe.wait_ge(mean_sb, B)
            nc.tensor.transpose(mean_bank[:, B * E:B * E + 2 * E * NT], gb_rows[:, :], ident[0:2 * E * NT, 0:2 * E * NT])
            mm(mean_bank[:, 0:B * E], ones_row[:, :], onehot_row[:, :, :].rearrange("p b e -> p (b e)"),
               start=True, stop=True).then_inc(onehot_ps, 1)

            pe.wait_ge(outT_sb, NT * B)
            pe.wait_ge(z_lo, NT * B)
            pe.wait_ge(adjT_lo, NT * B)
            pe.wait_ge(bn_chain, 2)
            for n in range(4 * NT):
                i, ht = n // NT, n % NT
                if ht == 0:
                    pe.wait_ge(raw_in[i], 16 * (J if i < 2 else 1))
                if n >= 8:
                    pe.wait_ge(w_lo, n - 7)
                for dt in range(NT):
                    ins = nc.tensor.transpose(bank[n % 8][:, dt * P:(dt + 1) * P],
                                              raw[i][:, dt, ht * P:(ht + 1) * P], ident[:, :])
                ins.then_inc(w_ps, 1)

            def y_rows(b, t):
                pe.wait_ge(yT_relu, NT * b + NT)
                for kt in range(NT):
                    ins = nc.tensor.transpose(t_bank[1][:, kt * P:(kt + 1) * P],
                                              yT[:, kt, t * P:(t + 1) * P], ident[:, :])
                ins.then_inc(y_ps, 1)

            def x1_transpose(b, t):
                pe.wait_ge(x1_done, NT * b + NT)
                for nt in range(NT):
                    ins = nc.tensor.transpose(t_bank[t % 2][:, nt * P:(nt + 1) * P],
                                              z[:, nt, t * P:(t + 1) * P], ident[:, :])
                ins.then_inc(xT_ps, 1)

            def dense(kind, b, i, half):
                if kind == "o" and half == 0:
                    pe.wait_ge(oT_lo, NT * b + NT)
                for t in (2 * half, 2 * half + 1):
                    if kind == "v" and i == 0:
                        pe.wait_ge(xT_lo, NT * b + t + 1)
                    for n, (a, c) in enumerate(PARTS):
                        if kind in "kq":
                            w, m = wT[kind][a][:, t, i * P:(i + 1) * P], xT[c][:, t, :]
                        elif kind == "v":
                            w, m = xT[a][:, t, i * P:(i + 1) * P], wT["v"][c][:, t, :]
                        else:
                            w, m = oT[a][:, t, i * P:(i + 1) * P], wT["o"][c][:, t, :]
                        ins = mm(dense_bank[:, :], w, m, start=(t == 0 and n == 0), stop=(t == NT - 1 and n == 2))
                if half == 1:
                    ins.then_inc(dense_ps[kind], 1)

            def scores(b, s):
                g, t = s // NT, s % NT
                if t == 0:
                    for m in "kq":
                        pe.wait_ge(packed[m], 64 * (NT * b + g + 1))
                need(pe, s_max, 64 * b + J * s)
                for j in range(J):
                    mm(s_bank[j][:, :], qp[:, g % 2, j, t * P:(t + 1) * P], kp[:, g % 2, j, :],
                       start=True, stop=True).then_inc(s_ps, 1)

            def weigh_v(b, s, par):
                g, t = s // NT, s % NT
                if s == 0:
                    pe.wait_ge(v_done, NT * b + NT)
                if t == 0:
                    need(pe, o_norm, G * b + g)
                pe.wait_ge(pT_act, 48 * b + 3 * s + 3)
                pe.wait_ge(pT_dve, 16 * b + s + 1)
                for mt in range(NT):
                    for j in range(J):
                        c = (g * J + j) * HD
                        ins = mm(pv_bank[j * HD:(j + 1) * HD, t * P:(t + 1) * P], v[:, par, mt, c:c + HD],
                                 probT[:, j, mt, :], start=(mt == 0), stop=(mt == NT - 1), skip_group_check=True)
                ins.then_inc(pv_ps, 1)

            def spread_recip(b, g):
                pe.wait_ge(wide_done, G * b + g + 1)
                for t in range(NT):
                    ins = nc.tensor.transpose(t_bank[0][:, t * P:(t + 1) * P],
                                              recip_wide[:, J * t:J * t + J, :].rearrange("p a d -> p (a d)"),
                                              ident[:, :])
                ins.then_inc(r_ps, 1)

            def prob_transpose(b, s, j):
                pe.wait_ge(exp_done, 64 * b + J * s + j + 1)
                for mt in range(NT):
                    ins = nc.tensor.transpose(t_bank[j % 2][:, mt * P:(mt + 1) * P],
                                              prob[:, s % 2, j, mt * P:(mt + 1) * P], ident[:, :])
                ins.then_inc(p_ps, 1)

            def t_bank_freed(n, b, s):
                need(pe, pT_act, 48 * b + 3 * s - (1 - n))

            pe.wait_ge(w_lo, 4 * NT)
            for t in range(NT):
                need(pe, y_sum, t)
                y_rows(0, t)
            pe.wait_ge(y_sum, NT)
            for t in range(NT):
                need(pe, xT_lo, t - 1)
                x1_transpose(0, t)
            order = [("v", i) for i in range(NT)] + [("k", 0), ("q", 0), ("k", 1), ("q", 1)]
            for n, (kind, i) in enumerate(order):
                if n > 0:
                    pe.wait_ge(freed[order[n - 1][0]], order[n - 1][1] + 1)
                dense(kind, 0, i, 0)
                dense(kind, 0, i, 1)
            pe.wait_ge(xT_lo, NT)
            scores(0, 0)

            def batch(b, par, first, last):
                prev = ("q", 1, 0)
                for s in range(STEPS):
                    if s + 1 < STEPS:
                        scores(b, s + 1)
                    elif not last:
                        scores(b + 1, 0)
                    if s > 0:
                        weigh_v(b, s - 1, par)
                    elif not first:
                        weigh_v(b - 1, STEPS - 1, 1 - par)
                    t_bank_freed(0, b, s)
                    t_bank_freed(1, b, s)
                    if s % NT == 0 and not (first and s == 0):
                        if s == 0:
                            spread_recip(b - 1, G - 1)
                            pe.wait_ge(r_sb, G * b)
                        else:
                            spread_recip(b, s // NT - 1)
                            pe.wait_ge(r_sb, G * b + s // NT)
                    if Y_STEP <= s < Y_STEP + NT and not last:
                        y_rows(b + 1, s - Y_STEP)
                    if s == XT_STEP and not last:
                        for t in range(NT):
                            if t >= 2:
                                pe.wait_ge(xT_lo, NT * (b + 1) + t - 1)
                            x1_transpose(b + 1, t)
                    kind, i, rel = SLOTS[s]
                    there = is_live(s, first, last)

                    def dense_half(half):
                        if not there:
                            return
                        if half == 0:
                            pe.wait_ge(freed[prev[0]], NT * (b + prev[2]) + prev[1] + 1)
                        dense(kind, b + rel, i, half)

                    def probs(js):
                        for j in js:
                            if j == 0 and s == XT_STEP and not last:
                                pe.wait_ge(xT_lo, NT * (b + 1) + 3)
                            if j == 1 and Y_STEP <= s < Y_STEP + NT and not last:
                                pe.wait_ge(y_sum, NT * (b + 1) + s - Y_STEP + 1)
                            if j == 1 and s == XT_STEP and not last:
                                pe.wait_ge(xT_lo, NT * (b + 1) + 4)
                            if j == 2:
                                pe.wait_ge(pT_act, 48 * b + 3 * s + 1)
                            if j == 3:
                                pe.wait_ge(pT_dve, 16 * b + s + 1)
                            prob_transpose(b, s, j)

                    if s in (0, XT_STEP):
                        probs((0, 1))
                        probs((2, 3))
                        dense_half(0)
                        dense_half(1)
                    else:
                        dense_half(0)
                        probs((0, 1))
                        dense_half(1)
                        probs((2, 3))
                    if there:
                        prev = (kind, i, rel)

            iterations(pe, batch)
            weigh_v(B - 1, STEPS - 1, 1)
            pe.wait_ge(pT_act, 48 * B - 1)
            spread_recip(B - 1, G - 1)
            for i in range(NT):
                if i > 0:
                    pe.wait_ge(f_sum, NT * (B - 1) + i)
                else:
                    pe.wait_ge(stage_lo["q"], NT * B)
                dense("o", B - 1, i, 0)
                dense("o", B - 1, i, 1)

        @block.scalar
        def _(act):
            def copy(dst, src, scale=1.0):
                return nc.scalar.activation(dst, src, ACT.Copy, scale=scale)

            def split_x(b):
                act.wait_ge(x_in, 16 * b + 16)
                need(act, z_ps, NT * b)
                copy(x_part[0][:, :, :], x_raw[:, :, :]).then_inc(x_hi, 1)

            def adjT_high(b):
                need(act, z_ps, NT * b)
                for t in range(NT):
                    act.wait_ge(adjT_ps, NT * b + t + 1)
                    copy(adjT[0][:, t, :], adjT_bank[t][:, :]).then_inc(adjT_hi, 1)

            def pick_expert(b, part):
                if part == 0:
                    wait_apart(act, route, 5 * b + 4)
                    pick_expert.no = act.value_load(index8[0:1, 0:1], min_val=0, max_val=E - 1)
                need(act, outT_ps, NT * b)
                src = f32(w_exp[part][:, bass.ds(pick_expert.no, 1), :, :]).rearrange("p o t n -> p (o t) n")
                copy(w_sel[part][:, :, :], src).then_inc(sel_lo if part else sel_hi, 1)

            def z_high(b, t):
                act.wait_ge(z_ps, NT * b + t + 1)
                need(act, outT_ps, NT * b)
                copy(zT[0][:, t, :], dense0_bank[t % 2][:, :]).then_inc(z_hi, 1)

            def z_and_expert(b):
                z_high(b, 0)
                pick_expert(b, 0)
                z_high(b, 1)
                pick_expert(b, 1)
                z_high(b, 2)
                z_high(b, 3)

            def copy_outT(b):
                for t in range(NT):
                    act.wait_ge(outT_ps, NT * b + t + 1)
                    if t == 0:
                        need(act, outT_spilled, 16 * b)
                        need(act, outT_st, NT * b)
                    copy(outT[:, t, :], dense0_bank[t % 2][:, :]).then_inc(outT_sb, 1)

            split_x(0)
            adjT_high(0)
            for e in range(E):
                act.wait_ge(experts_in, 16 * e + 16)
                copy(w_exp[0][:, e, :, :], raw[e][:, :, :]).then_inc(experts_hi, 1)
            act.wait_ge(experts_lo, E)
            z_and_expert(0)
            def batch0(b):
                adjT_high(b + 1)
                split_x(b + 1)
                copy_outT(b)
                z_and_expert(b + 1)

            batch0(0)
            with act.Fori(1, B - 1) as b:
                batch0(b)
            copy_outT(B - 1)

            layer0_over(act)
            for n in range(4 * NT):
                m, ht = "kqvo"[n // NT], n % NT
                act.wait_ge(w_ps, n + 1)
                copy(wT[m][0][:, ht, :], bank[n % 8][:, :], QSCALE if m == "q" else 1.0).then_inc(w_hi, 1)

            def relu_yT(b, t):
                if t == 0:
                    act.wait_ge(yT_in, 16 * b + 16)
                nc.scalar.activation(yT[:, t, :], yT[:, t, :], ACT.Relu,
                                     bias=bn_bias[:, bass.ds(b, 1), t:t + 1].rearrange("p o c -> p (o c)"),
                                     scale=bn_scale[:, bass.ds(b, 1), t:t + 1].rearrange("p o c -> p (o c)")).then_inc(yT_relu, 1)

            def xT_high(b, t):
                act.wait_ge(xT_ps, NT * b + t + 1)
                need(act, dense_ps["q"], NT * b)
                copy(xT[0][:, t, :], t_bank[t % 2][:, :]).then_inc(xT_hi, 1)

            def dense_out(kind, b, i, par):
                act.wait_ge(dense_ps[kind], NT * b + i + 1)
                if kind == "v":
                    need(act, pv_ps, 16 * (b - 1))
                    copy(v[:, par, i, :], dense_bank[:, :]).then_inc(v_done, 1)
                else:
                    need(act, packed[kind], 64 * (NT * b + i))
                    copy(stage[kind][0][:, :], dense_bank[:, :]).then_inc(stage_hi[kind], 1)

            def exp(b, s, j):
                g, t = s // NT, s % NT
                if j == 0:
                    act.wait_ge(neg_done, 16 * b + s + 1)
                    if t == 0:
                        need(act, wide_done, G * b + g - 1)
                nc.scalar.activation(prob[:, s % 2, j, :], prob[:, s % 2, j, :], ACT.Exp, scale=2.0,
                                     bias=neg_max[:, s % 2, j:j + 1],
                                     accum_out=row_sum[:, g % 2, J * t + j:J * t + j + 1]).then_inc(exp_done, 1)

            def copy_probT(b, s, j):
                act.wait_ge(p_ps, 64 * b + J * s + j + 1)
                copy(probT[:, j, :, :].rearrange("p a n -> p (a n)"), t_bank[j % 2][:, :]).then_inc(pT_act, 1)

            def copy_recip(b, g):
                act.wait_ge(r_ps, G * b + g + 1)
                need(act, oT_lo, G * b + g)
                copy(recip[:, :], t_bank[0][:, :]).then_inc(r_sb, 1)

            def oT_high(b, g):
                act.wait_ge(o_norm, G * b + g + 1)
                if g == 0:
                    need(act, dense_ps["o"], NT * b)
                copy(oT[0][:, g, :], recip[:, :]).then_inc(oT_hi, 1)

            act.wait_ge(bn_ready, 1)
            for t in range(NT):
                relu_yT(0, t)
            for t in range(NT):
                xT_high(0, t)
            for i in range(NT):
                dense_out("v", 0, i, 0)
            for i in range(2):
                dense_out("k", 0, i, 0)
                dense_out("q", 0, i, 0)
            for j in range(J):
                exp(0, 0, j)

            def batch(b, par, first, last):
                for s in range(STEPS):
                    nb, ns = (b, s + 1) if s + 1 < STEPS else (b + 1, 0)
                    ahead = not (last and ns == 0)
                    group_end = s % NT == 0 and not (first and s == 0)
                    gb, gg = (b, s // NT - 1) if s > 0 else (b - 1, G - 1)
                    if group_end:
                        copy_recip(gb, gg)
                    if s == XT_STEP and not last:
                        for t in range(NT):
                            xT_high(b + 1, t)
                    copy_probT(b, s, 0)
                    if ahead:
                        exp(nb, ns, 0)
                        exp(nb, ns, 1)
                    if group_end:
                        oT_high(gb, gg)
                    copy_probT(b, s, 2)
                    copy_probT(b, s, 3)
                    if ahead:
                        exp(nb, ns, 2)
                        exp(nb, ns, 3)
                    if s in (2, 3) and not last:
                        relu_yT(b + 1, 2 * (s - 2))
                        relu_yT(b + 1, 2 * (s - 2) + 1)
                    kind, i, rel = SLOTS[s]
                    if kind != "o" and is_live(s, first, last):
                        dense_out(kind, b + rel, i, 1 - par)

            iterations(act, batch)
            copy_recip(B - 1, G - 1)
            oT_high(B - 1, G - 1)

        @block.vector
        def _(dve):
            tt = nc.vector.tensor_tensor

            def low(dst, ps, hi):
                return tt(dst, ps, f32(hi), ALU.subtract)

            def sum_x(b):
                dve.wait_ge(x_in, 16 * b + 16)
                need(dve, mean_ps, b)
                tt(x_sum[:, :], x_raw[:, 0, :], x_raw[:, 1, :], ALU.add).then_inc(x_added, 1)
                for t in (2, 3):
                    dve.wait_ge(x_added, 3 * b + t - 1)
                    tt(x_sum[:, :], x_sum[:, :], x_raw[:, t, :], ALU.add).then_inc(x_added, 1)

            def adjT_low(b):
                need(dve, z_ps, NT * b)
                for t in range(NT):
                    dve.wait_ge(adjT_hi, NT * b + t + 1)
                    low(adjT[1][:, t, :], adjT_bank[t][:, :], adjT[0][:, t, :]).then_inc(adjT_lo, 1)

            def mean_copy(b):
                dve.wait_ge(mean_ps, b + 1)
                need(dve, score_ps, b)
                nc.vector.tensor_copy(x_mean[:, :], mean_bank[:, 0:NT]).then_inc(mean_sb, 1)

            def pick(b):
                n = 5 * b
                dve.wait_ge(score_ps, b + 1)
                tt(score8[:, 0:E], score_bank[0:1, 0:E], rb[:, :], ALU.add).then_inc(route, 1)
                wait_apart(dve, route, n + 1)
                nc.vector.max(best8[:, :], score8[:, :]).then_inc(route, 1)
                wait_apart(dve, route, n + 2)
                wait_apart(dve, sel_lo, b)
                nc.vector.max_index(index8[:, :], best8[:, :], score8[:, :]).then_inc(route, 1)
                dve.wait_ge(route, n + 3)
                nc.vector.tensor_copy(indexf[:, :], index8[:, :]).then_inc(route, 1)
                dve.wait_ge(route, n + 4)
                nc.vector.tensor_scalar(onehot_row[:, bass.ds(b, 1), :].rearrange("p o e -> p (o e)"),
                                        expert_no[:, :], indexf[:, 0:1], None, ALU.is_equal).then_inc(route, 1)

            def z_low(b):
                need(dve, outT_ps, NT * b)
                for t in range(NT):
                    dve.wait_ge(z_hi, NT * b + t + 1)
                    low(zT[1][:, t, :], dense0_bank[t % 2][:, :], zT[0][:, t, :]).then_inc(z_lo, 1)

            def out_stats(b, t):
                dve.wait_ge(outT_sb, NT * b + t + 1)
                nc.vector.bn_stats(st_bn[:, t, :], outT[:, t, :]).then_inc(outT_st, 1)
                wait_apart(dve, outT_st, NT * b + t + 1)
                if t == 0:
                    wait_apart(dve, outT_kept, b)
                nc.vector.bn_aggr(mv_now[:, t, :], st_bn[:, t, :]).then_inc(outT_mv, 1)

            def keep_stats(b):
                dve.wait_ge(outT_mv, NT * b + NT)
                nc.vector.tensor_copy(mv[:, bass.ds(b, 1), :].rearrange("p o c -> p (o c)"),
                                      mv_now[:, :, :].rearrange("p t c -> p (t c)")).then_inc(outT_kept, 1)

            dve.wait_ge(consts_made, 5 + E)
            sum_x(0)
            adjT_low(0)
            dve.wait_ge(small_in, 16 * 4)
            mean_copy(0)
            pick(0)
            for e in range(E):
                dve.wait_ge(experts_hi, e + 1)
                tt(w_exp[1][:, e, :, :], raw[e][:, :, :], f32(w_exp[0][:, e, :, :]), ALU.subtract).then_inc(experts_lo, 1)
            z_low(0)
            def batch0(b):
                adjT_low(b + 1)
                sum_x(b + 1)
                out_stats(b, 0)
                out_stats(b, 1)
                mean_copy(b + 1)
                out_stats(b, 2)
                pick(b + 1)
                out_stats(b, 3)
                keep_stats(b)
                z_low(b + 1)

            batch0(0)
            with dve.Fori(1, B - 1) as b:
                batch0(b)
            for t in range(NT):
                out_stats(B - 1, t)
            keep_stats(B - 1)

            chain = [0]

            def link(ins):
                chain[0] += 1
                ins.then_inc(bn_chain, 1)
                dve.wait_ge(bn_chain, chain[0])

            mean_b = mv[:, :, :].rearrange("p b (t c) -> p b t c", c=2)[:, :, :, 0]
            var_b = mv[:, :, :].rearrange("p b (t c) -> p b t c", c=2)[:, :, :, 1]
            dve.wait_ge(onehot_ps, 1)
            dve.wait_ge(outT_kept, B)
            link(nc.vector.tensor_copy(onehot[:, :, :].rearrange("p b e -> p (b e)"), mean_bank[:, 0:B * E]))
            link(nc.vector.tensor_copy(gam_bet[:, :, :, :].rearrange("p n e t -> p (n e t)"),
                                       mean_bank[:, B * E:B * E + 2 * E * NT]))
            link(tt(ex2[:, :, :], mean_b, mean_b, ALU.mult))
            link(tt(ex2[:, :, :], ex2[:, :, :], var_b, ALU.add))
            link(nc.vector.tensor_reduce(inv_cnt[:, :], onehot[:, :, :].rearrange("p b e -> p e b"), AX.X, ALU.add))
            link(nc.vector.tensor_scalar(inv_cnt[:, :], inv_cnt[:, :], 1.0 / N, None, ALU.max))
            link(nc.vector.reciprocal(inv_cnt[:, :], inv_cnt[:, :]))
            wide = [P, E, NT, B]
            pick_e = onehot[:, :, :].rearrange("p b (e o) -> p e o b", o=1).broadcast_to(wide)
            prod_e = prod[:, :].rearrange("p (e t b) -> p e t b", e=E, t=NT)
            for src, dst in ((mean_b, sum1), (ex2[:, :, :], sum2)):
                link(tt(prod_e, src.rearrange("p b (o t) -> p o t b", o=1).broadcast_to(wide), pick_e, ALU.mult))
                link(nc.vector.tensor_reduce(dst[:, :, :], prod_e, AX.X, ALU.add))
                link(tt(dst[:, :, :], dst[:, :, :],
                        inv_cnt[:, :].rearrange("p (e o) -> p e o", o=1).broadcast_to([P, E, NT]), ALU.mult))
            link(tt(scale_e[:, :, :], sum1[:, :, :], sum1[:, :, :], ALU.mult))
            link(tt(sum2[:, :, :], sum2[:, :, :], scale_e[:, :, :], ALU.subtract))
            link(nc.vector.tensor_scalar(sum2[:, :, :], sum2[:, :, :], EPS, None, ALU.add))
            assert chain[0] == BN_VAR
            dve.wait_ge(bn_pow, 1)
            link(tt(scale_e[:, :, :], sum2[:, :, :], gam_bet[:, 0, :, :], ALU.mult))
            link(tt(bias_e[:, :, :], sum1[:, :, :], scale_e[:, :, :], ALU.mult))
            link(tt(bias_e[:, :, :], gam_bet[:, 1, :, :], bias_e[:, :, :], ALU.subtract))
            wide = [P, B, NT, E]
            pick_b = onehot[:, :, :].rearrange("p b (o e) -> p b o e", o=1).broadcast_to(wide)
            prod_b = prod[:, :].rearrange("p (b t e) -> p b t e", b=B, t=NT)
            for src, dst in ((scale_e, bn_scale), (bias_e, bn_bias)):
                link(tt(prod_b, src[:, :, :].rearrange("p e (o t) -> p o t e", o=1).broadcast_to(wide), pick_b, ALU.mult))
                link(nc.vector.tensor_reduce(dst[:, :, :], prod_b, AX.X, ALU.add))
            nc.vector.memset(veps[:, :, :, :], 1.0).then_inc(bn_ready, 1)

            layer0_over(dve)
            for n in range(4 * NT):
                m, ht = "kqvo"[n // NT], n % NT
                dve.wait_ge(w_hi, n + 1)
                if m == "q":
                    ins = nc.vector.scalar_tensor_tensor(out=wT[m][1][:, ht, :], in0=bank[n % 8][:, :], scalar=QSCALE,
                                                         in1=f32(wT[m][0][:, ht, :]), op0=ALU.mult, op1=ALU.subtract)
                else:
                    ins = low(wT[m][1][:, ht, :], bank[n % 8][:, :], wT[m][0][:, ht, :])
                ins.then_inc(w_lo, 1)

            def norm_stats(which, b, t, sum_sem, st_sem, mv_sem, rstd_sem):
                dve.wait_ge(sum_sem, NT * b + t + 1)
                nc.vector.bn_stats(st_ln[:, which, t % 2, :], z[:, t, :]).then_inc(st_sem, 1)
                wait_apart(dve, st_sem, NT * b + t + 1)
                nc.vector.bn_aggr(mv_ln[:, which, t % 2, :], st_ln[:, which, t % 2, :]).then_inc(mv_sem, 1)

            def normalise(which, b, t, rstd_sem, done_sem):
                dve.wait_ge(rstd_sem, NT * b + t + 1)
                nc.vector.tensor_scalar(z[:, t, :], z[:, t, :], mv_ln[:, which, t % 2, 0:1],
                                        rstd[:, which, t % 2, 0:1], ALU.subtract, ALU.mult).then_inc(done_sem, 1)

            def add_y(b, t):
                dve.wait_ge(x1_x_in[t], 16 * b + 16)
                dve.wait_ge(y_ps, NT * b + t + 1)
                tt(z[:, t, :], t_bank[1][:, :], z[:, t, :], ALU.add).then_inc(y_sum, 1)

            def x1_stats(b, t):
                norm_stats(0, b, t, y_sum, y_st, y_mv, y_rstd)

            def x1_norm(b, t):
                normalise(0, b, t, y_rstd, x1_done)

            def xT_low(b, t):
                dve.wait_ge(xT_hi, NT * b + t + 1)
                low(xT[1][:, t, :], t_bank[t % 2][:, :], xT[0][:, t, :]).then_inc(xT_lo, 1)

            def stage_low(kind, b, i):
                dve.wait_ge(stage_hi[kind], NT * b + i + 1)
                low(stage[kind][1][:, :], dense_bank[:, :], stage[kind][0][:, :]).then_inc(stage_lo[kind], 1)

            def bias_and_max(b, s):
                g, t = s // NT, s % NT
                dve.wait_ge(adj1_in[t], 16 * b + 16)
                need(dve, p_ps, 64 * b + J * (s - 1))
                if t == 0:
                    need(dve, live_chain, 3 * (G * b + g - 1))
                for j in range(J):
                    wait_apart(dve, s_ps, 64 * b + J * s + j + 1)
                    nc.vector.tensor_tensor_reduce(prob[:, s % 2, j, :], s_bank[j][:, :], adj_sb[:, t, :], 1.0, LOWEST,
                                                   ALU.add, ALU.max,
                                                   row_max[:, g % 2, J * t + j:J * t + j + 1]).then_inc(s_max, 1)
                dve.wait_ge(s_max, 64 * b + J * s + J)
                need(dve, exp_done, 64 * b + J * (s - 1))
                nc.vector.tensor_scalar(neg_max[:, s % 2, :], row_max[:, g % 2, J * t:J * t + J], -2.0, None,
                                        ALU.mult).then_inc(neg_done, 1)

            def copy_probT(b, s, j):
                dve.wait_ge(p_ps, 64 * b + J * s + j + 1)
                nc.vector.tensor_copy(probT[:, j, :, :].rearrange("p a n -> p (a n)"),
                                      t_bank[j % 2][:, :]).then_inc(pT_dve, 1)

            def inverse_sum(b, g):
                dve.wait_ge(exp_done, 64 * b + 16 * g + 16)
                need(dve, wide_done, G * b + g)
                nc.vector.reciprocal(inv_sum[:, :], row_sum[:, g % 2, :]).then_inc(inv_half, 1)
                dve.wait_ge(live_chain, 3 * (G * b + g) + 3)
                dve.wait_ge(inv_half, 2 * (G * b + g) + 1)
                nc.vector.tensor_tensor(is_512[:, :], live[:, :], inv_sum[:, :], ALU.mult).then_inc(inv_half, 1)
                dve.wait_ge(inv_half, 2 * (G * b + g) + 2)
                nc.vector.tensor_tensor(inv_sum[:, :], inv_sum[:, :], is_512[:, :], ALU.subtract).then_inc(inv_done, 1)

            def weigh(b, g):
                dve.wait_ge(r_sb, G * b + g + 1)
                dve.wait_ge(pv_ps, 16 * b + NT * g + NT)
                tt(recip[:, :], pv_bank[:, :], recip[:, :], ALU.mult).then_inc(o_norm, 1)

            def oT_low(b, g):
                dve.wait_ge(oT_hi, G * b + g + 1)
                low(oT[1][:, g, :], recip[:, :], oT[0][:, g, :]).then_inc(oT_lo, 1)

            def add_residual(b, t):
                dve.wait_ge(x1_back, 16 * b + 16)
                dve.wait_ge(dense_ps["o"], NT * b + t + 1)
                tt(z[:, t, :], dense_bank[:, :], z[:, t, :], ALU.add).then_inc(f_sum, 1)

            def out_stats1(b, t):
                norm_stats(1, b, t, f_sum, f_st, f_mv, f_rstd)

            def out_norm(b, t):
                normalise(1, b, t, f_rstd, f_done)

            for t in range(NT):
                add_y(0, t)
                x1_stats(0, t)
                if t > 0:
                    x1_norm(0, t - 1)
            x1_norm(0, NT - 1)
            for t in range(NT):
                xT_low(0, t)
            for i in range(2):
                stage_low("k", 0, i)
                stage_low("q", 0, i)
            bias_and_max(0, 0)

            def batch(b, par, first, last):
                for s in range(STEPS):
                    if s + 1 < STEPS:
                        bias_and_max(b, s + 1)
                    elif not last:
                        bias_and_max(b + 1, 0)
                    if s % NT == 0 and not (first and s == 0):
                        gb, gg = (b, s // NT - 1) if s > 0 else (b - 1, G - 1)
                        weigh(gb, gg)
                    if s == XT_STEP and not last:
                        for t in range(NT):
                            xT_low(b + 1, t)
                    if Y_STEP <= s < Y_STEP + NT and not last:
                        add_y(b + 1, s - Y_STEP)
                    copy_probT(b, s, 1)
                    if s % NT == 0 and not (first and s == 0):
                        oT_low(gb, gg)
                    if Y_STEP <= s < Y_STEP + NT and not last:
                        x1_stats(b + 1, s - Y_STEP)
                    if 1 <= s <= 4 and not first:
                        out_norm(b - 1, s - 1)
                    kind, i, rel = SLOTS[s]
                    if s % NT == 3:
                        inverse_sum(b, s // NT)
                    if kind == "o" and not first:
                        add_residual(b - 1, i)
                        out_stats1(b - 1, i)
                    if kind in "kq" and is_live(s, first, last):
                        stage_low(kind, b + rel, i)
                    if Y_STEP <= s < Y_STEP + NT and not last:
                        x1_norm(b + 1, s - Y_STEP)

            iterations(dve, batch)
            weigh(B - 1, G - 1)
            oT_low(B - 1, G - 1)
            for t in range(NT):
                add_residual(B - 1, t)
                out_stats1(B - 1, t)
                out_norm(B - 1, t)


BN_VAR = 16

_INS = ["x", "adj", "L0_gnn_router_w", "L0_gnn_router_b", "L0_gnn_expert_w", "L0_gnn_bn_gamma", "L0_gnn_bn_beta",
        "L1_gnn_Wq", "L1_gnn_Wk", "L1_gnn_Wv", "L1_gnn_Wo"]


def kernel(**inputs):
    import numpy as _np
    import concourse.bacc as _bacc
    from concourse import mybir as _mybir
    from concourse.bass_utils import run_bass_kernel_spmd as _run

    nc = _bacc.Bacc("TRN2", target_bir_lowering=False, num_devices=1)
    arrays, args = {}, []
    for name in _INS:
        a = _np.ascontiguousarray(inputs[name])
        arrays[f"in_{name}_dram"] = a
        args.append(nc.dram_tensor(f"in_{name}_dram", a.shape, _mybir.dt.from_np(a.dtype), kind="ExternalInput").ap())
    args.append(nc.dram_tensor("out_0_dram", (B, N, H), _mybir.dt.from_np(_np.dtype("float32")),
                               kind="ExternalOutput").ap())
    gnn_program(nc, *args)
    r = _run(nc, [arrays], core_ids=[0])
    return r.results[0]["out_0_dram"]
```

```python
from contextlib import ExitStack

import concourse.bass as bass
from concourse import mybir

P = 128
ALU = mybir.AluOpType
ACT = mybir.ActivationFunctionType
AX = mybir.AxisListType
F32 = mybir.dt.float32
F32R = mybir.dt.float32r
U32 = mybir.dt.uint32

B, N, H = 16, 512, 512
NT = N // P
E = 4
HEADS, HD = 16, 32
G = HEADS // NT
J = 4
STEPS = G * NT
EPS = 1e-5
LOWEST = -3.0e38
QSCALE = float(H) ** -0.5 / 2.0
PARTS = ((0, 0), (0, 1), (1, 0))

SLOTS = ([("k", 2, 0)]
         + [("o", 0, -1), ("o", 1, -1), ("o", 2, -1), ("q", 2, 0), ("o", 3, -1), ("k", 3, 0), ("q", 3, 0)]
         + [("v", 0, 1), ("v", 1, 1), ("v", 2, 1), ("k", 0, 1), ("q", 0, 1), ("v", 3, 1), ("k", 1, 1), ("q", 1, 1)])
AHEAD = STEPS // 2
O_STEPS = {s: i for s, (kind, i, _) in enumerate(SLOTS) if kind == "o"}
O_ADDED = {s + 1: i for s, i in O_STEPS.items()}
O_NORMED = {s + 2: i for s, i in O_STEPS.items()}
Y_STEPS = {4: 0, 5: 1, 6: 2, 8: 3}
Y_NORMED = {s + 1: i for s, i in Y_STEPS.items()}
XT_EARLY, XT_MIDDLE = {8: 0, 9: 1}, {9: 2, 10: 3}
OT_STEPS = {0: 3, 6: 0, 8: 1, 12: 2}


def need(eng, sem, count):
    if not isinstance(count, int) or count > 0:
        eng.wait_ge(sem, count)


def f32(ap):
    return ap.bitcast(F32)


def gnn_program(nc, x, adj, router_w, router_b, expert_w, bn_gamma, bn_beta, Wq, Wk, Wv, Wo, out):
    outT_dram = nc.dram_tensor("outT_spill", [B, H, N], F32).ap()
    x1_dram = nc.dram_tensor("x1_spill", [B, N, H], F32).ap()

    def rows(dram, b):
        return dram[bass.ds(b, 1)].rearrange("o (t p) n -> p (o t) n", p=P)

    def row_tile(dram, b, t):
        return dram[bass.ds(b, 1), t * P:(t + 1) * P, :].rearrange("o p n -> p (o n)")

    with ExitStack() as ctx:
        sems = {}

        def sem(name):
            sems[name] = ctx.enter_context(nc.semaphore(name))
            return sems[name]

        def sb(stack, name, shape, dt=F32):
            return stack.enter_context(nc.sbuf_tensor(name, shape, dt))

        bank = [ctx.enter_context(nc.psum_tensor(f"bank{i}", [P, 512], F32)) for i in range(8)]

        ident = sb(ctx, "ident", [P, P])
        bn_scale = sb(ctx, "bn_scale", [P, B, NT])
        bn_bias = sb(ctx, "bn_bias", [P, B, NT])
        minus_half = sb(ctx, "minus_half", [P, 16])

        with ExitStack() as l0:
            w_exp = [sb(l0, f"w_exp{p}", [P, E, NT, H], F32R) for p in range(2)]
            raw = [sb(l0, f"w_raw{i}", [P, NT, H]) for i in range(4)]
            w_sel = [sb(l0, f"w_sel{p}", [P, NT, H], F32R) for p in range(2)]
            x_raw = sb(l0, "x_raw", [P, NT, H])
            adj_raw = sb(l0, "adj_raw", [P, NT, N])
            x_part = [sb(l0, f"x_part{p}", [P, NT, H], F32R) for p in range(2)]
            adjT = [sb(l0, f"adjT{p}", [P, NT, N], F32R) for p in range(2)]
            zT = [sb(l0, f"zT{p}", [P, NT, N], F32R) for p in range(2)]
            outT = sb(l0, "outT", [P, NT, N])
            x_sum = sb(l0, "x_sum", [P, H])
            inv_n = sb(l0, "inv_n", [P, 1])
            x_mean = sb(l0, "x_mean", [P, NT])
            rw = sb(l0, "rw", [P, NT, E])
            rb = sb(l0, "rb", [1, E])
            score8 = sb(l0, "score8", [1, 8])
            best8 = sb(l0, "best8", [1, 8])
            index8 = sb(l0, "index8", [1, 8], U32)
            indexf = sb(l0, "indexf", [1, 8])
            expert_no = sb(l0, "expert_no", [1, E])
            onehot_row = sb(l0, "onehot_row", [1, B, E])
            ones_row = sb(l0, "ones_row", [1, P])
            st_bn = sb(l0, "st_bn", [P, NT, 6])
            mv_now = sb(l0, "mv_now", [P, NT, 2])
            mv = sb(l0, "mv", [P, B, NT * 2])
            gb_rows = sb(l0, "gb_rows", [2 * E * NT, P])
            gam_bet = sb(l0, "gam_bet", [P, 2, E, NT])
            onehot = sb(l0, "onehot", [P, B, E])
            ex2 = sb(l0, "ex2", [P, B, NT])
            prod = sb(l0, "prod", [P, E * NT * B])
            sum1 = sb(l0, "sum1", [P, E, NT])
            sum2 = sb(l0, "sum2", [P, E, NT])
            inv_cnt = sb(l0, "inv_cnt", [P, E])
            scale_e = sb(l0, "scale_e", [P, E, NT])
            bias_e = sb(l0, "bias_e", [P, E, NT])

        with ExitStack() as l1:
            wT = {m: [sb(l1, f"w{m}T{p}", [P, NT, H], F32R) for p in range(2)] for m in "kqvo"}
            kp = sb(l1, "kp", [P, 2, J, N], F32R)
            qp = sb(l1, "qp", [P, 2, J, N], F32R)
            xT = [sb(l1, f"xT{p}", [P, NT, N], F32R) for p in range(2)]
            oT = [sb(l1, f"oT{p}", [P, NT, N], F32R) for p in range(2)]
            v = sb(l1, "v", [P, 2, NT, H])
            prob = sb(l1, "prob", [P, 2, J, N])
            probT = sb(l1, "probT", [P, J, NT, P])
            adj_sb = sb(l1, "adj_sb", [P, NT, N])
            yT = sb(l1, "yT", [P, NT, N])
            z = sb(l1, "z", [P, NT, H])
            stage = {m: [sb(l1, f"stage_{m}{p}", [P, N], F32R) for p in range(2)] for m in "kq"}
            recip = sb(l1, "recip", [P, N])
            recip_wide = sb(l1, "recip_wide", [P, NT * J, HD])
            row_max = sb(l1, "row_max", [P, 2, NT * J])
            row_sum = sb(l1, "row_sum", [P, 2, NT * J])
            neg_max = sb(l1, "neg_max", [P, 2, J])
            is_512 = sb(l1, "is_512", [P, NT * J])
            live = sb(l1, "live", [P, NT * J])
            inv_sum = sb(l1, "inv_sum", [P, NT * J])
            st_ln = sb(l1, "st_ln", [P, 2, 2, 6])
            mv_ln = sb(l1, "mv_ln", [P, 2, 2, 2])
            veps = sb(l1, "veps", [P, 2, 2, 1])
            rstd = sb(l1, "rstd", [P, 2, 2, 1])

        consts_made = sem("consts_made")
        ident_zero = sem("ident_zero")
        small_in = sem("small_in")
        experts_in = sem("experts_in")
        experts_hi = sem("experts_hi")
        experts_lo = sem("experts_lo")
        raw_in = [sem(f"raw_in{i}") for i in range(4)]
        adj_in = sem("adj_in")
        x_in = sem("x_in")
        adjT_ps = sem("adjT_ps")
        adjT_hi = sem("adjT_hi")
        adjT_lo = sem("adjT_lo")
        x_hi = sem("x_hi")
        x_lo = sem("x_lo")
        x_added = sem("x_added")
        mean_ps = sem("mean_ps")
        mean_sb = sem("mean_sb")
        score_ps = sem("score_ps")
        route = sem("route")
        sel_hi = sem("sel_hi")
        sel_lo = sem("sel_lo")
        z_ps = sem("z_ps")
        z_hi = sem("z_hi")
        z_lo = sem("z_lo")
        outT_ps = sem("outT_ps")
        outT_sb = sem("outT_sb")
        outT_st = sem("outT_st")
        outT_mv = sem("outT_mv")
        outT_kept = sem("outT_kept")
        outT_spilled = sem("outT_spilled")
        onehot_ps = sem("onehot_ps")
        bn_chain = sem("bn_chain")
        bn_pow = sem("bn_pow")
        bn_ready = sem("bn_ready")

        w_ps = sem("w_ps")
        w_hi = sem("w_hi")
        w_lo = sem("w_lo")
        adj1_in = [sem(f"adj1_in{t}") for t in range(NT)]
        yT_in = sem("yT_in")
        x1_x_in = [sem(f"x1_x_in{t}") for t in range(NT)]
        yT_relu = sem("yT_relu")
        y_ps = sem("y_ps")
        y_sum = sem("y_sum")
        y_st = sem("y_st")
        y_mv = sem("y_mv")
        y_eps = sem("y_eps")
        y_rstd = sem("y_rstd")
        x1_done = sem("x1_done")
        x1_spilled = sem("x1_spilled")
        x1_back = sem("x1_back")
        xT_ps = sem("xT_ps")
        xT_hi = sem("xT_hi")
        xT_lo = sem("xT_lo")
        dense_ps = {m: sem(f"dense_ps_{m}") for m in "kqvo"}
        stage_hi = {m: sem(f"stage_hi_{m}") for m in "kq"}
        stage_lo = {m: sem(f"stage_lo_{m}") for m in "kq"}
        packed = {m: sem(f"packed_{m}") for m in "kq"}
        v_done = sem("v_done")
        s_ps = sem("s_ps")
        s_max = sem("s_max")
        neg_done = sem("neg_done")
        exp_done = sem("exp_done")
        p_ps = sem("p_ps")
        pT_act = sem("pT_act")
        pT_dve = sem("pT_dve")
        pv_ps = sem("pv_ps")
        live_chain = sem("live_chain")
        inv_half = sem("inv_half")
        inv_done = sem("inv_done")
        wide_done = sem("wide_done")
        r_ps = sem("r_ps")
        r_sb = sem("r_sb")
        o_norm = sem("o_norm")
        oT_hi = sem("oT_hi")
        oT_lo = sem("oT_lo")
        f_sum = sem("f_sum")
        f_st = sem("f_st")
        f_mv = sem("f_mv")
        f_eps = sem("f_eps")
        f_rstd = sem("f_rstd")
        f_done = sem("f_done")
        out_stored = [sem(f"out_stored{t}") for t in range(NT)]

        freed = {"k": stage_lo["k"], "q": stage_lo["q"], "v": v_done, "o": f_sum}

        adjT_bank, dense0_bank, mean_bank, score_bank = bank[0:4], bank[4:6], bank[6], bank[7]
        s_bank = (bank[0], bank[1], bank[2], bank[0])
        dense_bank = (bank[3], bank[7])
        t_bank, pv_bank = bank[4:6], bank[6]

        def by_feature(ps):
            return ps[:, :].rearrange("p (h n) -> p h n", n=P)

        def y_bank(t):
            return dense_bank[(next(s for s, i in Y_STEPS.items() if i == t) + 1) % 2]

        def xT_bank(t):
            return dense_bank[t % 2]

        def wait_apart(eng, sem, count):
            if isinstance(count, int):
                need(eng, sem, count)
            else:
                count = eng.to_reg(count)
                eng.wait_ge(ident_zero, 1)
                eng.wait_ge(sem, count)

        def layer0_over(eng):
            eng.wait_ge(outT_ps, NT * B)
            eng.wait_ge(outT_sb, NT * B)
            eng.wait_ge(outT_kept, B)
            eng.wait_ge(outT_spilled, 16 * B)

        def iterations(eng, body):
            body(0, 0, True, False)
            with eng.Fori(0, B // 2 - 1) as i:
                body(i * 2 + 1, 1, False, False)
                body(i * 2 + 2, 0, False, False)
            body(B - 1, 1, False, True)

        def is_live(slot, first, last):
            rel = SLOTS[slot][2]
            return not (rel < 0 and first) and not (rel > 0 and last)

        block = ctx.enter_context(nc.Block())

        @block.sync
        def _(sp):
            def load0(b):
                wait_apart(sp, adjT_ps, NT * b)
                sp.dma_start(adj_raw[:, :, :], rows(adj, b)).then_inc(adj_in, 16)
                wait_apart(sp, x_lo, b)
                wait_apart(sp, x_hi, b)
                wait_apart(sp, x_added, 3 * b)
                sp.dma_start(x_raw[:, :, :], rows(x, b)).then_inc(x_in, 16)

            def spill_outT(b):
                wait_apart(sp, outT_sb, NT * b + NT)
                sp.dma_start(rows(outT_dram, b), outT[:, :, :]).then_inc(outT_spilled, 16)

            load0(0)
            for e in range(E):
                sp.dma_start(raw[e][:, :, :], expert_w[e].rearrange("(t p) n -> p t n", p=P)).then_inc(experts_in, 16)
            sp.dma_start(rw[:, :, :], router_w.rearrange("(t p) e -> p t e", p=P)).then_inc(small_in, 16)
            sp.dma_start(rb[:, :], router_b.rearrange("(o e) -> o e", o=1)).then_inc(small_in, 16)
            for n, w in enumerate((bn_gamma, bn_beta)):
                sp.dma_start(gb_rows[n * E * NT:(n + 1) * E * NT, :],
                             w.rearrange("e (t p) -> (e t) p", p=P)).then_inc(small_in, 16)
            load0(1)
            spill_outT(0)
            with sp.Fori(1, B - 1) as b:
                load0(b + 1)
                spill_outT(b)
            spill_outT(B - 1)

            def load_adj(b, t, reused):
                if reused:
                    wait_apart(sp, s_max, 64 * (b - 1) + J * (12 + t) + J)
                sp.dma_start(adj_sb[:, t, :], row_tile(adj, b, t)).then_inc(adj1_in[t], 16)

            def load_yT(b):
                wait_apart(sp, y_ps, NT * b)
                sp.dma_start(yT[:, :, :], rows(outT_dram, b)).then_inc(yT_in, 16)

            def pack(m, b, g):
                ring = g % 2
                wait_apart(sp, s_ps, 64 * b + 16 * (g - 1))
                wait_apart(sp, stage_lo[m], NT * b + g + 1)
                dst = kp if m == "k" else qp
                for part in range(4):
                    src = stage[m][(part % 2) if m == "k" else (part // 2)]
                    sp.dma_start(f32(dst[part * HD:(part + 1) * HD, ring, :, :]).rearrange("p j n -> p (j n)"),
                                 f32(src[:, :])).then_inc(packed[m], 16)

            def spill_x1(b):
                wait_apart(sp, x1_done, NT * b + NT)
                sp.dma_start(rows(x1_dram, b), z[:, :, :]).then_inc(x1_spilled, 16)

            def store_out(b, t):
                wait_apart(sp, f_done, NT * b + t + 1)
                sp.dma_start(row_tile(out, b, t), z[:, t, :]).then_inc(out_stored[t], 16)

            def load_x(b, t):
                sp.dma_start(z[:, t, :], row_tile(x, b, t)).then_inc(x1_x_in[t], 16)

            layer0_over(sp)
            load_yT(0)
            sp.wait_ge(bn_ready, 1)
            for t in range(NT):
                load_x(0, t)
            for t in range(NT):
                load_adj(0, t, False)
            spill_x1(0)
            for g in range(2):
                pack("k", 0, g)
                pack("q", 0, g)

            def batch(b, par, first, last):
                if not last:
                    load_yT(b + 1)
                for s in range(STEPS):
                    if s in O_NORMED and not first:
                        store_out(b - 1, O_NORMED[s])
                    if first and s == 1:
                        wait_apart(sp, x1_spilled, 16)
                        wait_apart(sp, xT_ps, NT)
                    if s in O_NORMED and not last:
                        if not first:
                            wait_apart(sp, out_stored[O_NORMED[s]], 16 * b)
                        load_x(b + 1, O_NORMED[s])
                    if last and s == 8:
                        for t in range(NT):
                            wait_apart(sp, out_stored[t], 16 * b)
                    kind, i, rel = SLOTS[s]
                    if s >= 12 and not last:
                        load_adj(b + 1, s - 12, True)
                    if kind in "kq" and is_live(s, first, last):
                        pack(kind, b + rel, i)
                    if s == 9 and not last:
                        spill_x1(b + 1)
                    if s == 11:
                        if not last:
                            wait_apart(sp, x1_spilled, 16 * (b + 2))
                            wait_apart(sp, xT_ps, NT * (b + 2))
                        sp.dma_start(z[:, :, :], rows(x1_dram, b)).then_inc(x1_back, 16)

            iterations(sp, batch)
            for t in range(NT):
                store_out(B - 1, t)
            for t in range(NT):
                wait_apart(sp, out_stored[t], 16 * B)

        @block.gpsimd
        def _(pool):
            nc.gpsimd.memset(ident[:, :], 0.0).then_inc(ident_zero, 1)
            pool.wait_ge(ident_zero, 1)
            nc.gpsimd.affine_select(out=ident[:, :], in_=ident[:, :], compare_op=ALU.not_equal, fill=1.0,
                                    base=0, pattern=[[-1, P]], channel_multiplier=1).then_inc(consts_made, 1)
            nc.gpsimd.memset(minus_half[:, :], -0.5).then_inc(consts_made, 1)
            nc.gpsimd.memset(inv_n[:, :], 1.0 / N).then_inc(consts_made, 1)
            nc.gpsimd.memset(ones_row[:, :], 1.0).then_inc(consts_made, 1)
            nc.gpsimd.memset(score8[:, :], LOWEST).then_inc(consts_made, 1)
            for e in range(E):
                nc.gpsimd.memset(expert_no[:, e:e + 1], float(e)).then_inc(consts_made, 1)

            def split_x(b):
                pool.wait_ge(x_hi, b + 1)
                need(pool, z_ps, NT * b)
                for t in range(NT):
                    ins = nc.gpsimd.tensor_tensor(x_part[1][:, t, :], x_raw[:, t, :], f32(x_part[0][:, t, :]),
                                                  ALU.subtract)
                ins.then_inc(x_lo, 1)

            split_x(0)
            pool.wait_ge(experts_lo, E)
            for i, w in enumerate((Wk, Wq)):
                by_head = w.rearrange("(t j d) n -> j d t n", j=J, d=HD)
                for j in range(J):
                    pool.dma_start(raw[i][j:P - J + j + 1:J, :, :], by_head[j]).then_inc(raw_in[i], 16)
            for i, w in ((2, Wv), (3, Wo)):
                pool.dma_start(raw[i][:, :, :], w.rearrange("(t p) n -> p t n", p=P)).then_inc(raw_in[i], 16)
            with pool.Fori(0, B - 1) as b:
                split_x(b + 1)

            pool.wait_ge(bn_chain, BN_VAR)
            nc.gpsimd.tensor_tensor(sum2[:, :, :].rearrange("p e t -> p (e t)"),
                                    sum2[:, :, :].rearrange("p e t -> p (e t)"),
                                    minus_half[:, :], ALU.pow).then_inc(bn_pow, 1)

            def layer_norm_rstd(which, b, t, mv_sem, eps_sem, rstd_sem):
                wait_apart(pool, mv_sem, NT * b + t + 1)
                nc.gpsimd.tensor_scalar(veps[:, which, t % 2, :], mv_ln[:, which, t % 2, 1:2], EPS, None,
                                        ALU.add).then_inc(eps_sem, 1)
                pool.wait_ge(eps_sem, NT * b + t + 1)
                nc.gpsimd.tensor_tensor(rstd[:, which, t % 2, :], veps[:, which, t % 2, :],
                                        minus_half[:, 0:1], ALU.pow).then_inc(rstd_sem, 1)

            def softmax_weights(b, g):
                ring = g % 2
                n = 3 * (G * b + g)
                wait_apart(pool, exp_done, 64 * b + 16 * g + 16)
                nc.gpsimd.tensor_scalar(is_512[:, :], row_sum[:, ring, :], float(N), None,
                                        ALU.is_equal).then_inc(live_chain, 1)
                nc.gpsimd.tensor_scalar(live[:, :], row_max[:, ring, :], 0.0, None,
                                        ALU.is_equal).then_inc(live_chain, 1)
                pool.wait_ge(live_chain, n + 2)
                nc.gpsimd.tensor_tensor(live[:, :], live[:, :], is_512[:, :], ALU.mult).then_inc(live_chain, 1)
                wait_apart(pool, live_chain, n + 3)
                wait_apart(pool, inv_done, G * b + g + 1)
                wait_apart(pool, r_ps, G * b + g)
                nc.gpsimd.tensor_scalar(recip_wide[:, :, :],
                                        inv_sum[:, :].rearrange("p (a o) -> p a o", o=1).broadcast_to([P, NT * J, HD]),
                                        1.0, None, ALU.mult).then_inc(wide_done, 1)

            for t in range(NT):
                layer_norm_rstd(0, 0, t, y_mv, y_eps, y_rstd)

            def batch(b, par, first, last):
                for s in range(STEPS):
                    if s % NT == 3:
                        softmax_weights(b, s // NT)
                    if s in O_ADDED and not first:
                        layer_norm_rstd(1, b - 1, O_ADDED[s], f_mv, f_eps, f_rstd)
                    if s in Y_STEPS and not last:
                        layer_norm_rstd(0, b + 1, Y_STEPS[s], y_mv, y_eps, y_rstd)

            iterations(pool, batch)
            for t in range(NT):
                layer_norm_rstd(1, B - 1, t, f_mv, f_eps, f_rstd)

        @block.tensor
        def _(pe):
            mm = nc.tensor.matmul

            def transpose_adj(b):
                pe.wait_ge(adj_in, 16 * b + 16)
                need(pe, adjT_lo, NT * b)
                for mt in range(NT):
                    for nt in range(NT):
                        ins = nc.tensor.transpose(adjT_bank[mt][:, nt * P:(nt + 1) * P],
                                                  adj_raw[:, nt, mt * P:(mt + 1) * P], ident[:, :])
                    ins.then_inc(adjT_ps, 1)

            def z_tiles(b):
                pe.wait_ge(x_lo, b + 1)
                for i in range(NT):
                    if i < 2:
                        need(pe, outT_sb, NT * (b - 1) + 3 + i)
                    else:
                        pe.wait_ge(z_lo, NT * b + i - 1)
                    ps = dense0_bank[i % 2]
                    for mt in range(NT):
                        if i == 0:
                            pe.wait_ge(adjT_lo, NT * b + mt + 1)
                        for n, (a, c) in enumerate(PARTS):
                            ins = mm(ps[:, :], x_part[a][:, mt, i * P:(i + 1) * P], adjT[c][:, mt, :],
                                     start=(mt == 0 and n == 0), stop=(mt == NT - 1 and n == 2))
                    ins.then_inc(z_ps, 1)

            def out_tile(b, i):
                if i == 0:
                    pe.wait_ge(sel_lo, b + 1)
                if i < 2:
                    pe.wait_ge(z_lo, NT * b + 3 + i)
                else:
                    pe.wait_ge(outT_sb, NT * b + i - 1)
                if i == 0:
                    pe.wait_ge(z_lo, NT * b + NT)
                ps = dense0_bank[i % 2]
                for ht in range(NT):
                    for n, (a, c) in enumerate(PARTS):
                        ins = mm(ps[:, :], w_sel[a][:, ht, i * P:(i + 1) * P], zT[c][:, ht, :],
                                 start=(ht == 0 and n == 0), stop=(ht == NT - 1 and n == 2))
                ins.then_inc(outT_ps, 1)

            def x_mean_product(b):
                pe.wait_ge(x_added, 3 * b + 3)
                need(pe, mean_sb, b)
                for t in range(NT):
                    ins = mm(mean_bank[:, t:t + 1], x_sum[:, t * P:(t + 1) * P], inv_n[:, :], start=True, stop=True)
                ins.then_inc(mean_ps, 1)

            def score_product(b):
                pe.wait_ge(mean_sb, b + 1)
                need(pe, route, 5 * b)
                for t in range(NT):
                    ins = mm(score_bank[0:1, 0:E], x_mean[:, t:t + 1], rw[:, t, :], start=(t == 0), stop=(t == NT - 1))
                ins.then_inc(score_ps, 1)

            pe.wait_ge(consts_made, 5 + E)
            pe.wait_ge(small_in, 16 * 4)
            transpose_adj(0)
            x_mean_product(0)
            score_product(0)
            z_tiles(0)
            def batch0(b):
                transpose_adj(b + 1)
                out_tile(b, 0)
                out_tile(b, 1)
                x_mean_product(b + 1)
                out_tile(b, 2)
                score_product(b + 1)
                out_tile(b, 3)
                z_tiles(b + 1)

            batch0(0)
            with pe.Fori(1, B - 1) as b:
                batch0(b)
            for i in range(NT):
                out_tile(B - 1, i)

            pe.wait_ge(route, 5 * B)
            pe.wait_ge(mean_sb, B)
            nc.tensor.transpose(mean_bank[:, B * E:B * E + 2 * E * NT], gb_rows[:, :], ident[0:2 * E * NT, 0:2 * E * NT])
            mm(mean_bank[:, 0:B * E], ones_row[:, :], onehot_row[:, :, :].rearrange("p b e -> p (b e)"),
               start=True, stop=True).then_inc(onehot_ps, 1)

            pe.wait_ge(outT_sb, NT * B)
            pe.wait_ge(z_lo, NT * B)
            pe.wait_ge(adjT_lo, NT * B)
            pe.wait_ge(bn_chain, 2)
            for n in range(4 * NT):
                i, ht = n // NT, n % NT
                if ht == 0:
                    pe.wait_ge(raw_in[i], 16 * (J if i < 2 else 1))
                if n >= 8:
                    pe.wait_ge(w_lo, n - 7)
                for dt in range(NT):
                    ins = nc.tensor.transpose(bank[n % 8][:, dt * P:(dt + 1) * P],
                                              raw[i][:, dt, ht * P:(ht + 1) * P], ident[:, :])
                ins.then_inc(w_ps, 1)

            def y_rows(b, t):
                pe.wait_ge(yT_relu, NT * b + NT)
                for kt in range(NT):
                    ins = nc.tensor.transpose(y_bank(t)[:, kt * P:(kt + 1) * P],
                                              yT[:, kt, t * P:(t + 1) * P], ident[:, :])
                ins.then_inc(y_ps, 1)

            def x1_transpose(b, t):
                pe.wait_ge(x1_done, NT * b + t + 1)
                for ht in range(NT):
                    ins = nc.tensor.transpose(xT_bank(t)[:, ht * P:(ht + 1) * P],
                                              z[:, t, ht * P:(ht + 1) * P], ident[:, :])
                ins.then_inc(xT_ps, 1)

            def dense(kind, b, i, half, ps):
                if kind == "o" and i == 0 and half == 0:
                    pe.wait_ge(oT_lo, NT * b + NT)
                if kind == "v" and half == 0:
                    pe.wait_ge(xT_lo, NT * b + i + 1)
                if kind == "k" and i == 0 and half == 0:
                    pe.wait_ge(xT_lo, NT * b + NT)
                for t in (2 * half, 2 * half + 1):
                    for n, (a, c) in enumerate(PARTS):
                        if kind in "kq":
                            w, m = wT[kind][a][:, t, i * P:(i + 1) * P], xT[c][:, t, :]
                        elif kind == "v":
                            w, m = xT[a][:, t, i * P:(i + 1) * P], wT["v"][c][:, t, :]
                        else:
                            w, m = oT[a][:, t, i * P:(i + 1) * P], wT["o"][c][:, t, :]
                        ins = mm(ps[:, :], w, m, start=(t == 0 and n == 0), stop=(t == NT - 1 and n == 2))
                if half == 1:
                    ins.then_inc(dense_ps[kind], 1)

            def scores(b, s, heads):
                g, t = s // NT, s % NT
                if t == 0 and heads[0] == 0:
                    for m in "kq":
                        pe.wait_ge(packed[m], 64 * (NT * b + g + 1))
                if heads[0] == 0:
                    need(pe, s_max, 64 * b + J * s)
                else:
                    pe.wait_ge(s_max, 64 * b + J * s + 1)
                for j in heads:
                    mm(s_bank[j][:, :], qp[:, g % 2, j, t * P:(t + 1) * P], kp[:, g % 2, j, :],
                       start=True, stop=True).then_inc(s_ps, 1)

            def weigh_v(b, s, par):
                g, t = s // NT, s % NT
                if s == 0:
                    pe.wait_ge(v_done, NT * b + NT)
                if t == 0:
                    need(pe, o_norm, G * b + g)
                pe.wait_ge(pT_act, 48 * b + 3 * s + 3)
                pe.wait_ge(pT_dve, 16 * b + s + 1)
                for mt in range(NT):
                    for j in range(J):
                        c = (g * J + j) * HD
                        ins = mm(pv_bank[j * HD:(j + 1) * HD, t * P:(t + 1) * P], v[:, par, mt, c:c + HD],
                                 probT[:, j, mt, :], start=(mt == 0), stop=(mt == NT - 1), skip_group_check=True)
                ins.then_inc(pv_ps, 1)

            def spread_recip(b, g):
                pe.wait_ge(wide_done, G * b + g + 1)
                for t in range(NT):
                    ins = nc.tensor.transpose(t_bank[0][:, t * P:(t + 1) * P],
                                              recip_wide[:, J * t:J * t + J, :].rearrange("p a d -> p (a d)"),
                                              ident[:, :])
                ins.then_inc(r_ps, 1)

            def prob_transpose(b, s, j):
                pe.wait_ge(exp_done, 64 * b + J * s + j + 1)
                for mt in range(NT):
                    ins = nc.tensor.transpose(t_bank[j % 2][:, mt * P:(mt + 1) * P],
                                              prob[:, s % 2, j, mt * P:(mt + 1) * P], ident[:, :])
                ins.then_inc(p_ps, 1)

            def t_bank_freed(n, b, s):
                if n == 0:
                    need(pe, pT_act, 48 * b + 3 * s)
                else:
                    need(pe, pT_dve, 16 * b + s)

            pe.wait_ge(w_lo, 4 * NT)
            for t in range(NT):
                need(pe, y_sum, t)
                y_rows(0, t)
            pe.wait_ge(y_sum, NT)
            for t in range(NT):
                need(pe, xT_lo, t - 1)
                x1_transpose(0, t)
            for s in range(AHEAD, STEPS):
                kind, i, _ = SLOTS[s]
                if s < AHEAD + 2:
                    pe.wait_ge(xT_lo, NT - 1 + s - AHEAD)
                else:
                    pe.wait_ge(freed[SLOTS[s - 2][0]], SLOTS[s - 2][1] + 1)
                for half in range(2):
                    dense(kind, 0, i, half, dense_bank[s % 2])
            scores(0, 0, (0, 1, 2))
            scores(0, 0, (3,))

            def batch(b, par, first, last):
                reader = [(freed[SLOTS[s][0]], NT * b + SLOTS[s][1] + 1) for s in (STEPS - 2, STEPS - 1)]
                for s in range(STEPS):
                    kind, i, rel = SLOTS[s]
                    there = is_live(s, first, last)
                    other = (s + 1) % 2
                    group_end = s % NT == 0 and not (first and s == 0)
                    late = s in XT_EARLY

                    def next_scores(heads):
                        if s + 1 < STEPS:
                            scores(b, s + 1, heads)
                        elif not last:
                            scores(b + 1, 0, heads)

                    def dense_half(half):
                        if there:
                            if half == 0:
                                pe.wait_ge(*reader[s % 2])
                            dense(kind, b + rel, i, half, dense_bank[s % 2])

                    next_scores((0, 1, 2))
                    if group_end:
                        t_bank_freed(0, b, s)
                        spread_recip(b if s else b - 1, s // NT - 1 if s else G - 1)
                    if s in XT_EARLY and not last:
                        pe.wait_ge(*reader[s % 2])
                        x1_transpose(b + 1, XT_EARLY[s])
                        reader[s % 2] = (xT_lo, NT * (b + 1) + XT_EARLY[s] + 1)
                    if not late:
                        dense_half(0)
                    next_scores((3,))
                    if s > 0:
                        weigh_v(b, s - 1, par)
                    elif not first:
                        weigh_v(b - 1, STEPS - 1, 1 - par)
                    if group_end:
                        pe.wait_ge(r_sb, G * b + s // NT)
                    if not group_end:
                        t_bank_freed(0, b, s)
                    prob_transpose(b, s, 0)
                    t_bank_freed(1, b, s)
                    prob_transpose(b, s, 1)
                    if s in Y_STEPS and not last:
                        pe.wait_ge(*reader[other])
                        y_rows(b + 1, Y_STEPS[s])
                        reader[other] = (y_sum, NT * (b + 1) + Y_STEPS[s] + 1)
                    if s in XT_MIDDLE and not last:
                        pe.wait_ge(*reader[other])
                        x1_transpose(b + 1, XT_MIDDLE[s])
                        reader[other] = (xT_lo, NT * (b + 1) + XT_MIDDLE[s] + 1)
                    if not late:
                        dense_half(1)
                    pe.wait_ge(pT_act, 48 * b + 3 * s + 1)
                    prob_transpose(b, s, 2)
                    pe.wait_ge(pT_act, 48 * b + 3 * s + 2)
                    prob_transpose(b, s, 3)
                    if late:
                        dense_half(0)
                        dense_half(1)
                    if there:
                        reader[s % 2] = (freed[kind], NT * (b + rel) + i + 1)

            iterations(pe, batch)
            pe.wait_ge(pT_act, 48 * B)
            spread_recip(B - 1, G - 1)
            weigh_v(B - 1, STEPS - 1, 1)
            for i in range(NT):
                if i > 1:
                    pe.wait_ge(f_sum, NT * (B - 1) + i - 1)
                else:
                    pe.wait_ge(stage_lo["q"], NT * B)
                dense("o", B - 1, i, 0, dense_bank[i % 2])
                dense("o", B - 1, i, 1, dense_bank[i % 2])

        @block.scalar
        def _(act):
            def copy(dst, src, scale=1.0):
                return nc.scalar.activation(dst, src, ACT.Copy, scale=scale)

            def split_x(b):
                act.wait_ge(x_in, 16 * b + 16)
                need(act, z_ps, NT * b)
                copy(x_part[0][:, :, :], x_raw[:, :, :]).then_inc(x_hi, 1)

            def adjT_high(b):
                need(act, z_ps, NT * b)
                for t in range(NT):
                    act.wait_ge(adjT_ps, NT * b + t + 1)
                    copy(adjT[0][:, t, :], adjT_bank[t][:, :]).then_inc(adjT_hi, 1)

            def pick_expert(b, part):
                if part == 0:
                    wait_apart(act, route, 5 * b + 4)
                    pick_expert.no = act.value_load(index8[0:1, 0:1], min_val=0, max_val=E - 1)
                need(act, outT_ps, NT * b)
                src = f32(w_exp[part][:, bass.ds(pick_expert.no, 1), :, :]).rearrange("p o t n -> p (o t) n")
                copy(w_sel[part][:, :, :], src).then_inc(sel_lo if part else sel_hi, 1)

            def z_high(b, t):
                act.wait_ge(z_ps, NT * b + t + 1)
                need(act, outT_ps, NT * b)
                copy(zT[0][:, t, :], dense0_bank[t % 2][:, :]).then_inc(z_hi, 1)

            def z_and_expert(b):
                z_high(b, 0)
                pick_expert(b, 0)
                z_high(b, 1)
                pick_expert(b, 1)
                z_high(b, 2)
                z_high(b, 3)

            def copy_outT(b):
                for t in range(NT):
                    act.wait_ge(outT_ps, NT * b + t + 1)
                    if t == 0:
                        need(act, outT_spilled, 16 * b)
                        need(act, outT_st, NT * b)
                    copy(outT[:, t, :], dense0_bank[t % 2][:, :]).then_inc(outT_sb, 1)

            split_x(0)
            adjT_high(0)
            for e in range(E):
                act.wait_ge(experts_in, 16 * e + 16)
                copy(w_exp[0][:, e, :, :], raw[e][:, :, :]).then_inc(experts_hi, 1)
            act.wait_ge(experts_lo, E)
            z_and_expert(0)
            def batch0(b):
                adjT_high(b + 1)
                split_x(b + 1)
                copy_outT(b)
                z_and_expert(b + 1)

            batch0(0)
            with act.Fori(1, B - 1) as b:
                batch0(b)
            copy_outT(B - 1)

            layer0_over(act)
            for n in range(4 * NT):
                m, ht = "kqvo"[n // NT], n % NT
                act.wait_ge(w_ps, n + 1)
                copy(wT[m][0][:, ht, :], bank[n % 8][:, :], QSCALE if m == "q" else 1.0).then_inc(w_hi, 1)

            def relu_yT(b, t):
                if t == 0:
                    act.wait_ge(yT_in, 16 * b + 16)
                nc.scalar.activation(yT[:, t, :], yT[:, t, :], ACT.Relu,
                                     bias=bn_bias[:, bass.ds(b, 1), t:t + 1].rearrange("p o c -> p (o c)"),
                                     scale=bn_scale[:, bass.ds(b, 1), t:t + 1].rearrange("p o c -> p (o c)")).then_inc(yT_relu, 1)

            def xT_high(b, t):
                act.wait_ge(xT_ps, NT * b + t + 1)
                need(act, dense_ps["q"], NT * b)
                copy(xT[0][:, :, t * P:(t + 1) * P], by_feature(xT_bank(t))).then_inc(xT_hi, 1)

            def dense_out(s, b, par):
                kind, i, _ = SLOTS[s]
                ps = dense_bank[s % 2]
                act.wait_ge(dense_ps[kind], NT * b + i + 1)
                if kind == "v":
                    need(act, pv_ps, 16 * (b - 1))
                    copy(v[:, par, i, :], ps[:, :]).then_inc(v_done, 1)
                else:
                    need(act, packed[kind], 64 * (NT * b + i))
                    copy(stage[kind][0][:, :], ps[:, :]).then_inc(stage_hi[kind], 1)

            def exp(b, s, j):
                g, t = s // NT, s % NT
                if j == 0:
                    act.wait_ge(neg_done, 16 * b + s + 1)
                    if t == 0:
                        need(act, wide_done, G * b + g - 1)
                nc.scalar.activation(prob[:, s % 2, j, :], prob[:, s % 2, j, :], ACT.Exp, scale=2.0,
                                     bias=neg_max[:, s % 2, j:j + 1],
                                     accum_out=row_sum[:, g % 2, J * t + j:J * t + j + 1]).then_inc(exp_done, 1)

            def copy_probT(b, s, j):
                act.wait_ge(p_ps, 64 * b + J * s + j + 1)
                copy(probT[:, j, :, :].rearrange("p a n -> p (a n)"), t_bank[j % 2][:, :]).then_inc(pT_act, 1)

            def copy_recip(b, g):
                act.wait_ge(r_ps, G * b + g + 1)
                need(act, oT_lo, G * b + g)
                copy(recip[:, :], t_bank[0][:, :]).then_inc(r_sb, 1)

            def oT_high(b, g):
                act.wait_ge(o_norm, G * b + g + 1)
                if g == 0:
                    need(act, dense_ps["o"], NT * b)
                copy(oT[0][:, g, :], recip[:, :]).then_inc(oT_hi, 1)

            act.wait_ge(bn_ready, 1)
            for t in range(NT):
                relu_yT(0, t)
            for t in range(NT):
                xT_high(0, t)
            for s in range(AHEAD, STEPS):
                dense_out(s, 0, 0)
            for j in range(J):
                exp(0, 0, j)

            def batch(b, par, first, last):
                for s in range(STEPS):
                    nb, ns = (b, s + 1) if s + 1 < STEPS else (b + 1, 0)
                    ahead = not (last and ns == 0)
                    group_end = s % NT == 0 and not (first and s == 0)
                    gb, gg = (b, s // NT - 1) if s > 0 else (b - 1, G - 1)
                    if group_end:
                        copy_recip(gb, gg)
                    if s in XT_EARLY and not last:
                        xT_high(b + 1, XT_EARLY[s])
                    copy_probT(b, s, 0)
                    copy_probT(b, s, 1)
                    if s in OT_STEPS and not (first and s == 0):
                        oT_high(b if s else b - 1, OT_STEPS[s])
                    if ahead:
                        exp(nb, ns, 0)
                        exp(nb, ns, 1)
                    if s in XT_MIDDLE and not last:
                        xT_high(b + 1, XT_MIDDLE[s])
                    copy_probT(b, s, 2)
                    kind, i, rel = SLOTS[s]
                    if kind != "o" and is_live(s, first, last):
                        dense_out(s, b + rel, 1 - par)
                    if ahead:
                        exp(nb, ns, 2)
                        exp(nb, ns, 3)
                    if s in (2, 3) and not last:
                        relu_yT(b + 1, 2 * (s - 2))
                        relu_yT(b + 1, 2 * (s - 2) + 1)

            iterations(act, batch)
            copy_recip(B - 1, G - 1)
            oT_high(B - 1, G - 1)

        @block.vector
        def _(dve):
            tt = nc.vector.tensor_tensor

            def low(dst, ps, hi):
                return tt(dst, ps, f32(hi), ALU.subtract)

            def sum_x(b):
                dve.wait_ge(x_in, 16 * b + 16)
                need(dve, mean_ps, b)
                tt(x_sum[:, :], x_raw[:, 0, :], x_raw[:, 1, :], ALU.add).then_inc(x_added, 1)
                for t in (2, 3):
                    dve.wait_ge(x_added, 3 * b + t - 1)
                    tt(x_sum[:, :], x_sum[:, :], x_raw[:, t, :], ALU.add).then_inc(x_added, 1)

            def adjT_low(b):
                need(dve, z_ps, NT * b)
                for t in range(NT):
                    dve.wait_ge(adjT_hi, NT * b + t + 1)
                    low(adjT[1][:, t, :], adjT_bank[t][:, :], adjT[0][:, t, :]).then_inc(adjT_lo, 1)

            def mean_copy(b):
                dve.wait_ge(mean_ps, b + 1)
                need(dve, score_ps, b)
                nc.vector.tensor_copy(x_mean[:, :], mean_bank[:, 0:NT]).then_inc(mean_sb, 1)

            def pick(b):
                n = 5 * b
                dve.wait_ge(score_ps, b + 1)
                tt(score8[:, 0:E], score_bank[0:1, 0:E], rb[:, :], ALU.add).then_inc(route, 1)
                wait_apart(dve, route, n + 1)
                nc.vector.max(best8[:, :], score8[:, :]).then_inc(route, 1)
                wait_apart(dve, route, n + 2)
                wait_apart(dve, sel_lo, b)
                nc.vector.max_index(index8[:, :], best8[:, :], score8[:, :]).then_inc(route, 1)
                dve.wait_ge(route, n + 3)
                nc.vector.tensor_copy(indexf[:, :], index8[:, :]).then_inc(route, 1)
                dve.wait_ge(route, n + 4)
                nc.vector.tensor_scalar(onehot_row[:, bass.ds(b, 1), :].rearrange("p o e -> p (o e)"),
                                        expert_no[:, :], indexf[:, 0:1], None, ALU.is_equal).then_inc(route, 1)

            def z_low(b):
                need(dve, outT_ps, NT * b)
                for t in range(NT):
                    dve.wait_ge(z_hi, NT * b + t + 1)
                    low(zT[1][:, t, :], dense0_bank[t % 2][:, :], zT[0][:, t, :]).then_inc(z_lo, 1)

            def out_stats(b, t):
                dve.wait_ge(outT_sb, NT * b + t + 1)
                nc.vector.bn_stats(st_bn[:, t, :], outT[:, t, :]).then_inc(outT_st, 1)
                wait_apart(dve, outT_st, NT * b + t + 1)
                if t == 0:
                    wait_apart(dve, outT_kept, b)
                nc.vector.bn_aggr(mv_now[:, t, :], st_bn[:, t, :]).then_inc(outT_mv, 1)

            def keep_stats(b):
                dve.wait_ge(outT_mv, NT * b + NT)
                nc.vector.tensor_copy(mv[:, bass.ds(b, 1), :].rearrange("p o c -> p (o c)"),
                                      mv_now[:, :, :].rearrange("p t c -> p (t c)")).then_inc(outT_kept, 1)

            dve.wait_ge(consts_made, 5 + E)
            sum_x(0)
            adjT_low(0)
            dve.wait_ge(small_in, 16 * 4)
            mean_copy(0)
            pick(0)
            for e in range(E):
                dve.wait_ge(experts_hi, e + 1)
                tt(w_exp[1][:, e, :, :], raw[e][:, :, :], f32(w_exp[0][:, e, :, :]), ALU.subtract).then_inc(experts_lo, 1)
            z_low(0)
            def batch0(b):
                adjT_low(b + 1)
                sum_x(b + 1)
                out_stats(b, 0)
                out_stats(b, 1)
                mean_copy(b + 1)
                out_stats(b, 2)
                pick(b + 1)
                out_stats(b, 3)
                keep_stats(b)
                z_low(b + 1)

            batch0(0)
            with dve.Fori(1, B - 1) as b:
                batch0(b)
            for t in range(NT):
                out_stats(B - 1, t)
            keep_stats(B - 1)

            chain = [0]

            def link(ins):
                chain[0] += 1
                ins.then_inc(bn_chain, 1)
                dve.wait_ge(bn_chain, chain[0])

            mean_b = mv[:, :, :].rearrange("p b (t c) -> p b t c", c=2)[:, :, :, 0]
            var_b = mv[:, :, :].rearrange("p b (t c) -> p b t c", c=2)[:, :, :, 1]
            dve.wait_ge(onehot_ps, 1)
            dve.wait_ge(outT_kept, B)
            link(nc.vector.tensor_copy(onehot[:, :, :].rearrange("p b e -> p (b e)"), mean_bank[:, 0:B * E]))
            link(nc.vector.tensor_copy(gam_bet[:, :, :, :].rearrange("p n e t -> p (n e t)"),
                                       mean_bank[:, B * E:B * E + 2 * E * NT]))
            link(tt(ex2[:, :, :], mean_b, mean_b, ALU.mult))
            link(tt(ex2[:, :, :], ex2[:, :, :], var_b, ALU.add))
            link(nc.vector.tensor_reduce(inv_cnt[:, :], onehot[:, :, :].rearrange("p b e -> p e b"), AX.X, ALU.add))
            link(nc.vector.tensor_scalar(inv_cnt[:, :], inv_cnt[:, :], 1.0 / N, None, ALU.max))
            link(nc.vector.reciprocal(inv_cnt[:, :], inv_cnt[:, :]))
            wide = [P, E, NT, B]
            pick_e = onehot[:, :, :].rearrange("p b (e o) -> p e o b", o=1).broadcast_to(wide)
            prod_e = prod[:, :].rearrange("p (e t b) -> p e t b", e=E, t=NT)
            for src, dst in ((mean_b, sum1), (ex2[:, :, :], sum2)):
                link(tt(prod_e, src.rearrange("p b (o t) -> p o t b", o=1).broadcast_to(wide), pick_e, ALU.mult))
                link(nc.vector.tensor_reduce(dst[:, :, :], prod_e, AX.X, ALU.add))
                link(tt(dst[:, :, :], dst[:, :, :],
                        inv_cnt[:, :].rearrange("p (e o) -> p e o", o=1).broadcast_to([P, E, NT]), ALU.mult))
            link(tt(scale_e[:, :, :], sum1[:, :, :], sum1[:, :, :], ALU.mult))
            link(tt(sum2[:, :, :], sum2[:, :, :], scale_e[:, :, :], ALU.subtract))
            link(nc.vector.tensor_scalar(sum2[:, :, :], sum2[:, :, :], EPS, None, ALU.add))
            assert chain[0] == BN_VAR
            dve.wait_ge(bn_pow, 1)
            link(tt(scale_e[:, :, :], sum2[:, :, :], gam_bet[:, 0, :, :], ALU.mult))
            link(tt(bias_e[:, :, :], sum1[:, :, :], scale_e[:, :, :], ALU.mult))
            link(tt(bias_e[:, :, :], gam_bet[:, 1, :, :], bias_e[:, :, :], ALU.subtract))
            wide = [P, B, NT, E]
            pick_b = onehot[:, :, :].rearrange("p b (o e) -> p b o e", o=1).broadcast_to(wide)
            prod_b = prod[:, :].rearrange("p (b t e) -> p b t e", b=B, t=NT)
            for src, dst in ((scale_e, bn_scale), (bias_e, bn_bias)):
                link(tt(prod_b, src[:, :, :].rearrange("p e (o t) -> p o t e", o=1).broadcast_to(wide), pick_b, ALU.mult))
                link(nc.vector.tensor_reduce(dst[:, :, :], prod_b, AX.X, ALU.add))
            nc.vector.memset(veps[:, :, :, :], 1.0).then_inc(bn_ready, 1)

            layer0_over(dve)
            for n in range(4 * NT):
                m, ht = "kqvo"[n // NT], n % NT
                dve.wait_ge(w_hi, n + 1)
                if m == "q":
                    ins = nc.vector.scalar_tensor_tensor(out=wT[m][1][:, ht, :], in0=bank[n % 8][:, :], scalar=QSCALE,
                                                         in1=f32(wT[m][0][:, ht, :]), op0=ALU.mult, op1=ALU.subtract)
                else:
                    ins = low(wT[m][1][:, ht, :], bank[n % 8][:, :], wT[m][0][:, ht, :])
                ins.then_inc(w_lo, 1)

            def norm_stats(which, b, t, sum_sem, st_sem, mv_sem, rstd_sem):
                dve.wait_ge(sum_sem, NT * b + t + 1)
                nc.vector.bn_stats(st_ln[:, which, t % 2, :], z[:, t, :]).then_inc(st_sem, 1)
                wait_apart(dve, st_sem, NT * b + t + 1)
                nc.vector.bn_aggr(mv_ln[:, which, t % 2, :], st_ln[:, which, t % 2, :]).then_inc(mv_sem, 1)

            def normalise(which, b, t, rstd_sem, done_sem):
                dve.wait_ge(rstd_sem, NT * b + t + 1)
                nc.vector.tensor_scalar(z[:, t, :], z[:, t, :], mv_ln[:, which, t % 2, 0:1],
                                        rstd[:, which, t % 2, 0:1], ALU.subtract, ALU.mult).then_inc(done_sem, 1)

            def add_y(b, t):
                dve.wait_ge(x1_x_in[t], 16 * b + 16)
                dve.wait_ge(y_ps, NT * b + t + 1)
                tt(z[:, t, :], y_bank(t)[:, :], z[:, t, :], ALU.add).then_inc(y_sum, 1)

            def x1_stats(b, t):
                norm_stats(0, b, t, y_sum, y_st, y_mv, y_rstd)

            def x1_norm(b, t):
                normalise(0, b, t, y_rstd, x1_done)

            def xT_low(b, t):
                dve.wait_ge(xT_hi, NT * b + t + 1)
                low(xT[1][:, :, t * P:(t + 1) * P], by_feature(xT_bank(t)),
                    xT[0][:, :, t * P:(t + 1) * P]).then_inc(xT_lo, 1)

            def stage_low(s, b):
                kind, i, _ = SLOTS[s]
                dve.wait_ge(stage_hi[kind], NT * b + i + 1)
                low(stage[kind][1][:, :], dense_bank[s % 2][:, :], stage[kind][0][:, :]).then_inc(stage_lo[kind], 1)

            def bias_and_max(b, s, heads):
                g, t = s // NT, s % NT
                if heads[0] == 0:
                    dve.wait_ge(adj1_in[t], 16 * b + 16)
                    need(dve, p_ps, 64 * b + J * (s - 1))
                    if t == 0:
                        need(dve, live_chain, 3 * (G * b + g - 1))
                for j in heads:
                    wait_apart(dve, s_ps, 64 * b + J * s + j + 1)
                    nc.vector.tensor_tensor_reduce(prob[:, s % 2, j, :], s_bank[j][:, :], adj_sb[:, t, :], 1.0, LOWEST,
                                                   ALU.add, ALU.max,
                                                   row_max[:, g % 2, J * t + j:J * t + j + 1]).then_inc(s_max, 1)

            def negate_max(b, s):
                g, t = s // NT, s % NT
                dve.wait_ge(s_max, 64 * b + J * s + J)
                need(dve, exp_done, 64 * b + J * (s - 1))
                nc.vector.tensor_scalar(neg_max[:, s % 2, :], row_max[:, g % 2, J * t:J * t + J], -2.0, None,
                                        ALU.mult).then_inc(neg_done, 1)

            def copy_probT(b, s, j):
                dve.wait_ge(p_ps, 64 * b + J * s + j + 1)
                nc.vector.tensor_copy(probT[:, j, :, :].rearrange("p a n -> p (a n)"),
                                      t_bank[j % 2][:, :]).then_inc(pT_dve, 1)

            def inverse_sum(b, g):
                dve.wait_ge(exp_done, 64 * b + 16 * g + 16)
                need(dve, wide_done, G * b + g)
                nc.vector.reciprocal(inv_sum[:, :], row_sum[:, g % 2, :]).then_inc(inv_half, 1)
                dve.wait_ge(live_chain, 3 * (G * b + g) + 3)
                dve.wait_ge(inv_half, 2 * (G * b + g) + 1)
                nc.vector.tensor_tensor(is_512[:, :], live[:, :], inv_sum[:, :], ALU.mult).then_inc(inv_half, 1)
                dve.wait_ge(inv_half, 2 * (G * b + g) + 2)
                nc.vector.tensor_tensor(inv_sum[:, :], inv_sum[:, :], is_512[:, :], ALU.subtract).then_inc(inv_done, 1)

            def weigh(b, g):
                dve.wait_ge(r_sb, G * b + g + 1)
                dve.wait_ge(pv_ps, 16 * b + NT * g + NT)
                tt(recip[:, :], pv_bank[:, :], recip[:, :], ALU.mult).then_inc(o_norm, 1)

            def oT_low(b, g):
                dve.wait_ge(oT_hi, G * b + g + 1)
                low(oT[1][:, g, :], recip[:, :], oT[0][:, g, :]).then_inc(oT_lo, 1)

            def add_residual(b, t, ps):
                dve.wait_ge(x1_back, 16 * b + 16)
                dve.wait_ge(dense_ps["o"], NT * b + t + 1)
                tt(z[:, t, :], ps[:, :], z[:, t, :], ALU.add).then_inc(f_sum, 1)

            def out_stats1(b, t):
                norm_stats(1, b, t, f_sum, f_st, f_mv, f_rstd)

            def out_norm(b, t):
                normalise(1, b, t, f_rstd, f_done)

            for t in range(NT):
                add_y(0, t)
                x1_stats(0, t)
                if t > 0:
                    x1_norm(0, t - 1)
            x1_norm(0, NT - 1)
            for t in range(NT):
                xT_low(0, t)
            for s in range(AHEAD, STEPS):
                if SLOTS[s][0] != "v":
                    stage_low(s, 0)
            bias_and_max(0, 0, (0, 1, 2))
            bias_and_max(0, 0, (3,))
            negate_max(0, 0)

            def batch(b, par, first, last):
                for s in range(STEPS):
                    nb, ns = (b, s + 1) if s + 1 < STEPS else (b + 1, 0)
                    ahead = not (last and ns == 0)
                    group_end = s % NT == 0 and not (first and s == 0)
                    gb, gg = (b, s // NT - 1) if s > 0 else (b - 1, G - 1)
                    if s > 0:
                        copy_probT(b, s - 1, 3)
                    elif not first:
                        copy_probT(b - 1, STEPS - 1, 3)
                    if ahead:
                        bias_and_max(nb, ns, (0, 1, 2))
                    if s > 0:
                        (kind, i, rel), there = SLOTS[s - 1], is_live(s - 1, first, last)
                    else:
                        (kind, i, _), rel, there = SLOTS[STEPS - 1], 0, not first
                    if kind in "kq" and there:
                        stage_low((s - 1) % STEPS, b + rel)
                    if ahead:
                        bias_and_max(nb, ns, (3,))
                        negate_max(nb, ns)
                    if s % NT == 3:
                        inverse_sum(b, s // NT)
                    if kind == "o" and there:
                        add_residual(b - 1, i, dense_bank[(s - 1) % 2])
                        out_stats1(b - 1, i)
                    if s in O_NORMED and not first:
                        out_norm(b - 1, O_NORMED[s])
                    if s in Y_NORMED and not last:
                        x1_norm(b + 1, Y_NORMED[s])
                    if s in XT_EARLY and not last:
                        xT_low(b + 1, XT_EARLY[s])
                    if s > 1 and s - 1 in OT_STEPS:
                        oT_low(b, OT_STEPS[s - 1])
                    if group_end:
                        weigh(gb, gg)
                    if s == 0 and not first:
                        oT_low(b - 1, OT_STEPS[s])
                    if s in Y_STEPS and not last:
                        add_y(b + 1, Y_STEPS[s])
                        x1_stats(b + 1, Y_STEPS[s])
                    if s in XT_MIDDLE and not last:
                        xT_low(b + 1, XT_MIDDLE[s])

            iterations(dve, batch)
            copy_probT(B - 1, STEPS - 1, 3)
            weigh(B - 1, G - 1)
            oT_low(B - 1, G - 1)
            for t in range(NT):
                add_residual(B - 1, t, dense_bank[t % 2])
                out_stats1(B - 1, t)
                out_norm(B - 1, t)


BN_VAR = 16

_INS = ["x", "adj", "L0_gnn_router_w", "L0_gnn_router_b", "L0_gnn_expert_w", "L0_gnn_bn_gamma", "L0_gnn_bn_beta",
        "L1_gnn_Wq", "L1_gnn_Wk", "L1_gnn_Wv", "L1_gnn_Wo"]


def kernel(**inputs):
    import numpy as _np
    import concourse.bacc as _bacc
    from concourse import mybir as _mybir
    from concourse.bass_utils import run_bass_kernel_spmd as _run

    nc = _bacc.Bacc("TRN2", target_bir_lowering=False, num_devices=1)
    arrays, args = {}, []
    for name in _INS:
        a = _np.ascontiguousarray(inputs[name])
        arrays[f"in_{name}_dram"] = a
        args.append(nc.dram_tensor(f"in_{name}_dram", a.shape, _mybir.dt.from_np(a.dtype), kind="ExternalInput").ap())
    args.append(nc.dram_tensor("out_0_dram", (B, N, H), _mybir.dt.from_np(_np.dtype("float32")),
                               kind="ExternalOutput").ap())
    gnn_program(nc, *args)
    r = _run(nc, [arrays], core_ids=[0])
    return r.results[0]["out_0_dram"]
```

```python
from contextlib import ExitStack

import concourse.bass as bass
from concourse import mybir

P = 128
ALU = mybir.AluOpType
ACT = mybir.ActivationFunctionType
AX = mybir.AxisListType
F32 = mybir.dt.float32
F32R = mybir.dt.float32r
U32 = mybir.dt.uint32

B, N, H = 16, 512, 512
NT = N // P
E = 4
HEADS, HD = 16, 32
G = HEADS // NT
J = 4
STEPS = G * NT
EPS = 1e-5
LOWEST = -3.0e38
QSCALE = float(H) ** -0.5 / 2.0
PARTS = ((0, 0), (0, 1), (1, 0))

SLOTS = ([("k", 2, 0)]
         + [("o", 0, -1), ("o", 1, -1), ("o", 2, -1), ("q", 2, 0), ("o", 3, -1), ("k", 3, 0), ("q", 3, 0)]
         + [("v", 0, 1), ("v", 1, 1), ("v", 2, 1), ("k", 0, 1), ("q", 0, 1), ("v", 3, 1), ("k", 1, 1), ("q", 1, 1)])
AHEAD = STEPS // 2
O_STEPS = {s: i for s, (kind, i, _) in enumerate(SLOTS) if kind == "o"}
O_ADDED = {s + 1: i for s, i in O_STEPS.items()}
O_NORMED = {s + 2: i for s, i in O_STEPS.items()}
Y_STEPS = {4: 0, 5: 1, 6: 2, 8: 3}
RELU_STEPS = {1: (0,), 2: (1, 2), 3: (3,)}
Y_NORMED = {s + 1: i for s, i in Y_STEPS.items()}
XT_EARLY, XT_MIDDLE = {8: 0, 9: 1}, {9: 2, 10: 3}
OT_STEPS = {0: 3, 6: 0, 8: 1, 12: 2}


W_WITH_OUT = [range(i * 2, (i + 1) * 2) for i in range(NT)]
W_LATER = (range(2 * NT, 3 * NT), range(3 * NT, 4 * NT))


ACT_COPIES_3 = (3, 4, 5, 6)


def copies_act(b, s, n=0):
    return (3 * STEPS + len(ACT_COPIES_3)) * b + 3 * s + sum(x < s for x in ACT_COPIES_3) + n


def copies_dve(b, s):
    return (STEPS - len(ACT_COPIES_3)) * b + s - sum(x < s for x in ACT_COPIES_3)


def need(eng, sem, count):
    if not isinstance(count, int) or count > 0:
        eng.wait_ge(sem, count)


def f32(ap):
    return ap.bitcast(F32)


def gnn_program(nc, x, adj, router_w, router_b, expert_w, bn_gamma, bn_beta, Wq, Wk, Wv, Wo, out):
    outT_dram = nc.dram_tensor("outT_spill", [B, H, N], F32).ap()
    x1_dram = nc.dram_tensor("x1_spill", [B, N, H], F32).ap()

    def rows(dram, b):
        return dram[bass.ds(b, 1)].rearrange("o (t p) n -> p (o t) n", p=P)

    def row_tile(dram, b, t):
        return dram[bass.ds(b, 1), t * P:(t + 1) * P, :].rearrange("o p n -> p (o n)")

    with ExitStack() as ctx:
        sems = {}

        def sem(name):
            sems[name] = ctx.enter_context(nc.semaphore(name))
            return sems[name]

        def sb(stack, name, shape, dt=F32):
            return stack.enter_context(nc.sbuf_tensor(name, shape, dt))

        bank = [ctx.enter_context(nc.psum_tensor(f"bank{i}", [P, 512], F32)) for i in range(8)]

        ident = sb(ctx, "ident", [P, P])
        bn_scale = sb(ctx, "bn_scale", [P, B, NT])
        bn_bias = sb(ctx, "bn_bias", [P, B, NT])
        minus_half = sb(ctx, "minus_half", [P, 16])

        with ExitStack() as l0:
            w_exp = [sb(l0, f"w_exp{p}", [P, E, NT, H], F32R) for p in range(2)]
            raw = [sb(l0, f"w_raw{i}", [P, NT, H]) for i in range(4)]
            w_sel = [sb(l0, f"w_sel{p}", [P, NT, H], F32R) for p in range(2)]
            x_raw = sb(l0, "x_raw", [P, NT, H])
            adj_raw = sb(l0, "adj_raw", [P, NT, N])
            x_part = [sb(l0, f"x_part{p}", [P, NT, H], F32R) for p in range(2)]
            adjT = [sb(l0, f"adjT{p}", [P, NT, N], F32R) for p in range(2)]
            zT = [sb(l0, f"zT{p}", [P, NT, N], F32R) for p in range(2)]
            outT = sb(l0, "outT", [P, NT, N])
            x_sum = sb(l0, "x_sum", [P, H])
            inv_n = sb(l0, "inv_n", [P, 1])
            rw = sb(l0, "rw", [P, H, E])
            x_rw = sb(l0, "x_rw", [P, 2, H])
            score_part = sb(l0, "score_part", [P, E])
            rb = sb(l0, "rb", [1, E])
            score8 = sb(l0, "score8", [1, 8])
            best8 = sb(l0, "best8", [1, 8])
            index8 = sb(l0, "index8", [1, 8], U32)
            indexf = sb(l0, "indexf", [1, 8])
            expert_no = sb(l0, "expert_no", [1, E])
            onehot_row = sb(l0, "onehot_row", [1, B, E])
            ones_row = sb(l0, "ones_row", [1, P])
            st_bn = sb(l0, "st_bn", [P, NT, 6])
            mv_now = sb(l0, "mv_now", [P, NT, 2])
            mv = sb(l0, "mv", [P, B, NT * 2])
            gb_rows = sb(l0, "gb_rows", [2 * E * NT, P])
            gam_bet = sb(l0, "gam_bet", [P, 2, E, NT])
            onehot = sb(l0, "onehot", [P, B, E])
            ex2 = sb(l0, "ex2", [P, B, NT])
            prod = sb(l0, "prod", [P, E * NT * B])
            sum1 = sb(l0, "sum1", [P, E, NT])
            sum2 = sb(l0, "sum2", [P, E, NT])
            inv_cnt = sb(l0, "inv_cnt", [P, E])
            scale_e = sb(l0, "scale_e", [P, E, NT])
            bias_e = sb(l0, "bias_e", [P, E, NT])

        with ExitStack() as l1:
            wT = {m: [sb(l1, f"w{m}T{p}", [P, NT, H], F32R) for p in range(2)] for m in "kqvo"}
            kp = sb(l1, "kp", [P, 2, J, N], F32R)
            qp = sb(l1, "qp", [P, 2, J, N], F32R)
            xT = [sb(l1, f"xT{p}", [P, NT, N], F32R) for p in range(2)]
            oT = [sb(l1, f"oT{p}", [P, NT, N], F32R) for p in range(2)]
            v = sb(l1, "v", [P, 2, NT, H])
            prob = sb(l1, "prob", [P, 2, J, N])
            probT = sb(l1, "probT", [P, J, NT, 2 * P])
            adj_sb = sb(l1, "adj_sb", [P, NT, N])
            z = sb(l1, "z", [P, NT, H])
            stage = {m: [sb(l1, f"stage_{m}{p}", [P, N], F32R) for p in range(2)] for m in "kq"}
            recip = sb(l1, "recip", [P, N])
            recip_wide = sb(l1, "recip_wide", [P, NT * J, HD])
            row_max = sb(l1, "row_max", [P, 2, NT * J])
            row_sum = sb(l1, "row_sum", [P, 2, NT * J])
            neg_max = sb(l1, "neg_max", [P, 2, J])
            is_512 = sb(l1, "is_512", [P, NT * J])
            live = sb(l1, "live", [P, NT * J])
            inv_sum = sb(l1, "inv_sum", [P, NT * J])
            zeros_inv = sb(l1, "zeros_inv", [P, NT * J])
            st_ln = sb(l1, "st_ln", [P, 2, 2, 6])
            mv_ln = sb(l1, "mv_ln", [P, 2, 2, 2])
            veps = sb(l1, "veps", [P, 2, 2, 1])
            rstd = sb(l1, "rstd", [P, 2, 2, 1])

        consts_made = sem("consts_made")
        ident_zero = sem("ident_zero")
        router_in = sem("router_in")
        small_in = sem("small_in")
        experts_in = [sem(f"experts_in{e}") for e in range(E)]
        experts_hi = sem("experts_hi")
        experts_lo = sem("experts_lo")
        raw_in = [sem(f"raw_in{i}") for i in range(4)]
        adj_in = sem("adj_in")
        x_in = sem("x_in")
        adjT_ps = sem("adjT_ps")
        adjT_hi = sem("adjT_hi")
        adjT_lo = sem("adjT_lo")
        x_hi = sem("x_hi")
        x_lo = sem("x_lo")
        x_added = sem("x_added")
        scored = sem("scored")
        score_ps = sem("score_ps")
        route = sem("route")
        sel_hi = sem("sel_hi")
        sel_lo = sem("sel_lo")
        z_ps = sem("z_ps")
        z_hi = sem("z_hi")
        z_lo = sem("z_lo")
        outT_ps = sem("outT_ps")
        outT_sb = sem("outT_sb")
        outT_st = sem("outT_st")
        outT_mv = sem("outT_mv")
        outT_kept = sem("outT_kept")
        outT_spilled = sem("outT_spilled")
        onehot_ps = sem("onehot_ps")
        bn_chain = sem("bn_chain")
        bn_pow = sem("bn_pow")
        bn_ready = sem("bn_ready")

        w_ps = sem("w_ps")
        w_hi = sem("w_hi")
        w_lo = sem("w_lo")
        adj1_in = [sem(f"adj1_in{t}") for t in range(NT)]
        yT_in = sem("yT_in")
        x1_x_in = [sem(f"x1_x_in{t}") for t in range(NT)]
        yT_relu = sem("yT_relu")
        y_ps = sem("y_ps")
        y_sum = sem("y_sum")
        y_st = sem("y_st")
        y_mv = sem("y_mv")
        y_eps = sem("y_eps")
        y_rstd = sem("y_rstd")
        x1_done = sem("x1_done")
        x1_spilled = sem("x1_spilled")
        x1_back = sem("x1_back")
        xT_ps = sem("xT_ps")
        xT_hi = sem("xT_hi")
        xT_lo = sem("xT_lo")
        dense_ps = {m: sem(f"dense_ps_{m}") for m in "kqvo"}
        stage_hi = {m: sem(f"stage_hi_{m}") for m in "kq"}
        stage_lo = {m: sem(f"stage_lo_{m}") for m in "kq"}
        packed = {m: sem(f"packed_{m}") for m in "kq"}
        v_done = sem("v_done")
        s_ps = sem("s_ps")
        s_max = sem("s_max")
        neg_done = sem("neg_done")
        exp_done = sem("exp_done")
        p_ps = sem("p_ps")
        pT_act = sem("pT_act")
        pT_dve = sem("pT_dve")
        pv_ps = sem("pv_ps")
        live_chain = sem("live_chain")
        inv_half = sem("inv_half")
        inv_done = sem("inv_done")
        wide_done = sem("wide_done")
        r_ps = sem("r_ps")
        r_sb = sem("r_sb")
        o_norm = sem("o_norm")
        oT_hi = sem("oT_hi")
        oT_lo = sem("oT_lo")
        f_sum = sem("f_sum")
        f_st = sem("f_st")
        f_mv = sem("f_mv")
        f_eps = sem("f_eps")
        f_rstd = sem("f_rstd")
        f_done = sem("f_done")
        out_stored = [sem(f"out_stored{t}") for t in range(NT)]

        freed = {"k": stage_lo["k"], "q": stage_lo["q"], "v": v_done, "o": f_sum}

        adjT_bank, dense0_bank, onehot_bank, score_bank = bank[0:4], bank[4:6], bank[6], bank[7]
        s_bank = (bank[0], bank[1], bank[2], bank[0])
        dense_bank = (bank[3], bank[7])
        t_bank, pv_bank = bank[4:6], bank[6]

        def by_block(ps):
            return ps[:, :].rearrange("p (h n) -> p h n", n=P)

        first_y_bank = (bank[3], bank[0], bank[1], bank[2])
        first_xT_bank = (bank[7], bank[4], bank[5], bank[6])
        last_o_bank = (dense_bank[0], dense_bank[1], s_bank[1], s_bank[2])
        y_bank = {t: dense_bank[(s + 1) % 2] for s, t in Y_STEPS.items()}
        xT_bank = {t: dense_bank[s % 2] for s, t in XT_EARLY.items()}
        xT_bank.update({t: dense_bank[(s + 1) % 2] for s, t in XT_MIDDLE.items()})

        def wait_apart(eng, sem, count):
            if isinstance(count, int):
                need(eng, sem, count)
            else:
                count = eng.to_reg(count)
                eng.wait_ge(ident_zero, 1)
                eng.wait_ge(sem, count)

        def layer0_over(eng):
            eng.wait_ge(outT_ps, NT * B)
            eng.wait_ge(outT_sb, NT * B)
            eng.wait_ge(outT_kept, B)
            eng.wait_ge(outT_spilled, 16 * B)

        def iterations(eng, body):
            body(0, 0, True, False)
            with eng.Fori(0, B // 2 - 1) as i:
                body(i * 2 + 1, 1, False, False)
                body(i * 2 + 2, 0, False, False)
            body(B - 1, 1, False, True)

        def is_live(slot, first, last):
            rel = SLOTS[slot][2]
            return not (rel < 0 and first) and not (rel > 0 and last)

        block = ctx.enter_context(nc.Block())

        @block.sync
        def _(sp):
            def load0(b):
                wait_apart(sp, adjT_ps, NT * b)
                sp.dma_start(adj_raw[:, :, :], rows(adj, b)).then_inc(adj_in, 16)
                wait_apart(sp, x_lo, b)
                wait_apart(sp, x_hi, b)
                wait_apart(sp, x_added, 3 * b)
                sp.dma_start(x_raw[:, :, :], rows(x, b)).then_inc(x_in, 16)

            def spill_outT(b):
                wait_apart(sp, outT_sb, NT * b + NT)
                sp.dma_start(rows(outT_dram, b), outT[:, :, :]).then_inc(outT_spilled, 16)

            load0(0)
            for e in range(E):
                sp.dma_start(raw[e][:, :, :], expert_w[e].rearrange("(t p) n -> p t n", p=P)).then_inc(experts_in[e], 16)
                if e == 1:
                    sp.dma_start(rw[:, :, :].rearrange("p h e -> p (h e)"),
                                 router_w.rearrange("(o h) e -> o (h e)", o=1).broadcast_to([P, H * E])).then_inc(router_in, 16)
                    sp.dma_start(rb[:, :], router_b.rearrange("(o e) -> o e", o=1)).then_inc(router_in, 16)
            load0(1)
            for n, w in enumerate((bn_gamma, bn_beta)):
                sp.dma_start(gb_rows[n * E * NT:(n + 1) * E * NT, :],
                             w.rearrange("e (t p) -> (e t) p", p=P)).then_inc(small_in, 16)
            spill_outT(0)
            with sp.Fori(1, B - 1) as b:
                load0(b + 1)
                spill_outT(b)
            spill_outT(B - 1)

            def load_adj(b, t, reused):
                if reused:
                    wait_apart(sp, s_max, 64 * (b - 1) + J * (12 + t) + J)
                sp.dma_start(adj_sb[:, t, :], row_tile(adj, b, t)).then_inc(adj1_in[t], 16)

            def load_yT(b, par):
                wait_apart(sp, pv_ps, 8 * (b - 1))
                sp.dma_start(v[:, par, :, :], rows(outT_dram, b)).then_inc(yT_in, 16)

            def pack(m, b, g):
                ring = g % 2
                wait_apart(sp, s_ps, 64 * b + 16 * (g - 1))
                wait_apart(sp, stage_lo[m], NT * b + g + 1)
                dst = kp if m == "k" else qp
                for part in range(4):
                    src = stage[m][(part % 2) if m == "k" else (part // 2)]
                    sp.dma_start(f32(dst[part * HD:(part + 1) * HD, ring, :, :]).rearrange("p j n -> p (j n)"),
                                 f32(src[:, :])).then_inc(packed[m], 16)

            def spill_x1(b):
                wait_apart(sp, x1_done, NT * b + NT)
                sp.dma_start(rows(x1_dram, b), z[:, :, :]).then_inc(x1_spilled, 16)

            def store_out(b, t):
                wait_apart(sp, f_done, NT * b + t + 1)
                sp.dma_start(row_tile(out, b, t), z[:, t, :]).then_inc(out_stored[t], 16)

            def load_x(b, t):
                sp.dma_start(z[:, t, :], row_tile(x, b, t)).then_inc(x1_x_in[t], 16)

            layer0_over(sp)
            load_yT(0, 0)
            sp.wait_ge(bn_ready, 1)
            for t in range(NT):
                load_x(0, t)
            for t in range(NT):
                load_adj(0, t, False)
            spill_x1(0)
            for g in range(2):
                pack("k", 0, g)
                pack("q", 0, g)

            def batch(b, par, first, last):
                if not last:
                    load_yT(b + 1, 1 - par)
                for s in range(STEPS):
                    if s in O_NORMED and not first:
                        store_out(b - 1, O_NORMED[s])
                    if first and s == 1:
                        wait_apart(sp, x1_spilled, 16)
                        wait_apart(sp, xT_ps, NT)
                    if s in O_NORMED and not last:
                        if not first:
                            wait_apart(sp, out_stored[O_NORMED[s]], 16 * b)
                        load_x(b + 1, O_NORMED[s])
                    if last and s == 8:
                        for t in range(NT):
                            wait_apart(sp, out_stored[t], 16 * b)
                    kind, i, rel = SLOTS[s]
                    if s >= 12 and not last:
                        load_adj(b + 1, s - 12, True)
                    if kind in "kq" and is_live(s, first, last):
                        pack(kind, b + rel, i)
                    if s == 9 and not last:
                        spill_x1(b + 1)
                    if s == 11:
                        if not last:
                            wait_apart(sp, x1_spilled, 16 * (b + 2))
                            wait_apart(sp, xT_ps, NT * (b + 2))
                        sp.dma_start(z[:, :, :], rows(x1_dram, b)).then_inc(x1_back, 16)

            iterations(sp, batch)
            for t in range(NT):
                store_out(B - 1, t)
            for t in range(NT):
                wait_apart(sp, out_stored[t], 16 * B)

        @block.gpsimd
        def _(pool):
            nc.gpsimd.memset(ident[:, :], 0.0).then_inc(ident_zero, 1)
            pool.wait_ge(ident_zero, 1)
            nc.gpsimd.affine_select(out=ident[:, :], in_=ident[:, :], compare_op=ALU.not_equal, fill=1.0,
                                    base=0, pattern=[[-1, P]], channel_multiplier=1).then_inc(consts_made, 1)
            nc.gpsimd.memset(minus_half[:, :], -0.5).then_inc(consts_made, 1)
            nc.gpsimd.memset(inv_n[:, :], 1.0 / N).then_inc(consts_made, 1)
            nc.gpsimd.memset(ones_row[:, :], 1.0).then_inc(consts_made, 1)
            nc.gpsimd.memset(score8[:, :], LOWEST).then_inc(consts_made, 1)
            for e in range(E):
                nc.gpsimd.memset(expert_no[:, e:e + 1], float(e)).then_inc(consts_made, 1)

            def split_x(b):
                pool.wait_ge(x_hi, b + 1)
                need(pool, z_ps, NT * b)
                for t in range(NT):
                    ins = nc.gpsimd.tensor_tensor(x_part[1][:, t, :], x_raw[:, t, :], f32(x_part[0][:, t, :]),
                                                  ALU.subtract)
                ins.then_inc(x_lo, 1)

            for e, tiles in ((0, slice(0, NT)), (1, slice(0, NT)), (3, slice(NT // 2, NT))):
                pool.wait_ge(experts_hi, e + 1)
                nc.gpsimd.tensor_tensor(w_exp[1][:, e, tiles, :], raw[e][:, tiles, :], f32(w_exp[0][:, e, tiles, :]),
                                        ALU.subtract).then_inc(experts_lo, 1)
            split_x(1)
            pool.wait_ge(experts_lo, E + 1)
            for i, w in enumerate((Wk, Wq)):
                by_head = w.rearrange("(t j d) n -> j d t n", j=J, d=HD)
                for j in range(J):
                    pool.dma_start(raw[i][j:P - J + j + 1:J, :, :], by_head[j]).then_inc(raw_in[i], 16)
            for i, w in ((2, Wv), (3, Wo)):
                pool.dma_start(raw[i][:, :, :], w.rearrange("(t p) n -> p t n", p=P)).then_inc(raw_in[i], 16)
            with pool.Fori(1, B - 1) as b:
                split_x(b + 1)

            pool.wait_ge(bn_chain, BN_VAR)
            nc.gpsimd.tensor_tensor(sum2[:, :, :].rearrange("p e t -> p (e t)"),
                                    sum2[:, :, :].rearrange("p e t -> p (e t)"),
                                    minus_half[:, :], ALU.pow).then_inc(bn_pow, 1)

            def layer_norm_rstd(which, b, t, mv_sem, eps_sem, rstd_sem):
                wait_apart(pool, mv_sem, NT * b + t + 1)
                nc.gpsimd.tensor_scalar(veps[:, which, t % 2, :], mv_ln[:, which, t % 2, 1:2], EPS, None,
                                        ALU.add).then_inc(eps_sem, 1)
                pool.wait_ge(eps_sem, NT * b + t + 1)
                nc.gpsimd.tensor_tensor(rstd[:, which, t % 2, :], veps[:, which, t % 2, :],
                                        minus_half[:, 0:1], ALU.pow).then_inc(rstd_sem, 1)

            def softmax_weights(b, g):
                ring = g % 2
                n = 3 * (G * b + g)
                wait_apart(pool, exp_done, 64 * b + 16 * g + 16)
                nc.gpsimd.tensor_scalar(is_512[:, :], row_sum[:, ring, :], float(N), None,
                                        ALU.is_equal).then_inc(live_chain, 1)
                nc.gpsimd.tensor_scalar(live[:, :], row_max[:, ring, :], 0.0, None,
                                        ALU.is_equal).then_inc(live_chain, 1)
                pool.wait_ge(live_chain, n + 2)
                nc.gpsimd.tensor_tensor(live[:, :], live[:, :], is_512[:, :], ALU.mult).then_inc(live_chain, 1)
                wait_apart(pool, live_chain, n + 3)
                wait_apart(pool, inv_done, G * b + g + 1)
                wait_apart(pool, r_ps, G * b + g)
                wide = [P, NT * J, HD]
                nc.gpsimd.tensor_tensor(recip_wide[:, :, :],
                                        inv_sum[:, :].rearrange("p (a o) -> p a o", o=1).broadcast_to(wide),
                                        zeros_inv[:, :].rearrange("p (a o) -> p a o", o=1).broadcast_to(wide),
                                        ALU.subtract).then_inc(wide_done, 1)

            for t in range(NT):
                layer_norm_rstd(0, 0, t, y_mv, y_eps, y_rstd)

            def batch(b, par, first, last):
                for s in range(STEPS):
                    if s % NT == 3:
                        softmax_weights(b, s // NT)
                    if s in O_ADDED and not first:
                        layer_norm_rstd(1, b - 1, O_ADDED[s], f_mv, f_eps, f_rstd)
                    if s in Y_STEPS and not last:
                        layer_norm_rstd(0, b + 1, Y_STEPS[s], y_mv, y_eps, y_rstd)

            iterations(pool, batch)
            for t in range(NT):
                layer_norm_rstd(1, B - 1, t, f_mv, f_eps, f_rstd)

        @block.tensor
        def _(pe):
            mm = nc.tensor.matmul

            def transpose_adj(b):
                pe.wait_ge(adj_in, 16 * b + 16)
                need(pe, adjT_lo, NT * b)
                for mt in range(NT):
                    for nt in range(NT):
                        ins = nc.tensor.transpose(adjT_bank[mt][:, nt * P:(nt + 1) * P],
                                                  adj_raw[:, nt, mt * P:(mt + 1) * P], ident[:, :])
                    ins.then_inc(adjT_ps, 1)

            def z_tiles(b, with_score=False):
                pe.wait_ge(x_lo, b + 1)
                for i in range(NT):
                    if with_score and i == 3:
                        score_product(b)
                    if i < 2:
                        need(pe, outT_sb, NT * (b - 1) + 3 + i)
                    else:
                        pe.wait_ge(z_lo, NT * b + i - 1)
                    ps = dense0_bank[i % 2]
                    for mt in range(NT):
                        if i == 0:
                            pe.wait_ge(adjT_lo, NT * b + mt + 1)
                        for n, (a, c) in enumerate(PARTS):
                            ins = mm(ps[:, :], x_part[a][:, mt, i * P:(i + 1) * P], adjT[c][:, mt, :],
                                     start=(mt == 0 and n == 0), stop=(mt == NT - 1 and n == 2))
                    ins.then_inc(z_ps, 1)

            def out_tile(b, i):
                if i == 0:
                    pe.wait_ge(sel_lo, b + 1)
                if i < 2:
                    pe.wait_ge(z_lo, NT * b + 3 + i)
                else:
                    pe.wait_ge(outT_sb, NT * b + i - 1)
                if i == 0:
                    pe.wait_ge(z_lo, NT * b + NT)
                ps = dense0_bank[i % 2]
                for ht in range(NT):
                    for n, (a, c) in enumerate(PARTS):
                        ins = mm(ps[:, :], w_sel[a][:, ht, i * P:(i + 1) * P], zT[c][:, ht, :],
                                 start=(ht == 0 and n == 0), stop=(ht == NT - 1 and n == 2))
                ins.then_inc(outT_ps, 1)

            def score_product(b):
                pe.wait_ge(scored, E * b + E)
                need(pe, route, 5 * b)
                mm(score_bank[0:1, 0:E], inv_n[:, :], score_part[:, :], start=True, stop=True).then_inc(score_ps, 1)

            def weight_transpose(n):
                i, ht = n // NT, n % NT
                if ht == 0:
                    pe.wait_ge(raw_in[i], 16 * (J if i < 2 else 1))
                if n >= NT:
                    pe.wait_ge(w_lo, n - NT + 1)
                for dt in range(NT):
                    ins = nc.tensor.transpose(bank[n % NT][:, dt * P:(dt + 1) * P],
                                              raw[i][:, dt, ht * P:(ht + 1) * P], ident[:, :])
                ins.then_inc(w_ps, 1)

            pe.wait_ge(consts_made, 5 + E)
            transpose_adj(0)
            z_tiles(0, True)
            def batch0(b):
                transpose_adj(b + 1)
                out_tile(b, 0)
                out_tile(b, 1)
                out_tile(b, 2)
                score_product(b + 1)
                out_tile(b, 3)
                z_tiles(b + 1)

            batch0(0)
            with pe.Fori(1, B - 1) as b:
                batch0(b)
            pe.wait_ge(small_in, 16 * 2)
            pe.wait_ge(route, 5 * B)
            nc.tensor.transpose(onehot_bank[:, B * E:B * E + 2 * E * NT], gb_rows[:, :], ident[0:2 * E * NT, 0:2 * E * NT])
            mm(onehot_bank[:, 0:B * E], ones_row[:, :], onehot_row[:, :, :].rearrange("p b e -> p (b e)"),
               start=True, stop=True).then_inc(onehot_ps, 1)
            for i in range(NT):
                for n in W_WITH_OUT[i]:
                    weight_transpose(n)
                out_tile(B - 1, i)
            for tiles in W_LATER:
                for n in tiles:
                    weight_transpose(n)

            def y_rows(b, t, ps, par):
                pe.wait_ge(yT_relu, NT * b + NT)
                for kt in range(NT):
                    ins = nc.tensor.transpose(ps[:, kt * P:(kt + 1) * P],
                                              v[:, par, kt, t * P:(t + 1) * P], ident[:, :])
                ins.then_inc(y_ps, 1)

            def x1_transpose(b, t, ps):
                pe.wait_ge(x1_done, NT * b + t + 1)
                for ht in range(NT):
                    ins = nc.tensor.transpose(ps[:, ht * P:(ht + 1) * P],
                                              z[:, t, ht * P:(ht + 1) * P], ident[:, :])
                ins.then_inc(xT_ps, 1)

            def dense(kind, b, i, tiles, ps):
                if kind == "o" and i == 0:
                    pe.wait_ge(oT_lo, NT * b + tiles[-1] + 1)
                if kind == "v" and tiles[0] == 0:
                    pe.wait_ge(xT_lo, NT * b + i + 1)
                if kind == "k" and i == 0 and tiles[0] == 0:
                    pe.wait_ge(xT_lo, NT * b + NT)
                for t in tiles:
                    for n, (a, c) in enumerate(PARTS):
                        if kind in "kq":
                            w, m = wT[kind][a][:, t, i * P:(i + 1) * P], xT[c][:, t, :]
                        elif kind == "v":
                            w, m = xT[a][:, t, i * P:(i + 1) * P], wT["v"][c][:, t, :]
                        else:
                            w, m = oT[a][:, t, i * P:(i + 1) * P], wT["o"][c][:, t, :]
                        ins = mm(ps[:, :], w, m, start=(t == 0 and n == 0), stop=(t == NT - 1 and n == 2))
                if tiles[-1] == NT - 1:
                    ins.then_inc(dense_ps[kind], 1)

            def scores(b, s, heads):
                g, t = s // NT, s % NT
                if t == 0 and heads[0] == 0:
                    for m in "kq":
                        pe.wait_ge(packed[m], 64 * (NT * b + g + 1))
                if heads[0] == 0:
                    need(pe, s_max, 64 * b + J * s)
                else:
                    pe.wait_ge(s_max, 64 * b + J * s + 1)
                for j in heads:
                    mm(s_bank[j][:, :], qp[:, g % 2, j, t * P:(t + 1) * P], kp[:, g % 2, j, :],
                       start=True, stop=True).then_inc(s_ps, 1)

            def weigh_v(b, s, par):
                g, t = s // NT, s % NT
                if s == 1:
                    pe.wait_ge(v_done, NT * b + NT)
                if t == 1:
                    need(pe, o_norm, G * b + g)
                pe.wait_ge(pT_act, copies_act(b, s + 1))
                pe.wait_ge(pT_dve, copies_dve(b, s + 1))
                for mt in range(NT):
                    for j in range(J):
                        c = (g * J + j) * HD
                        ins = mm(pv_bank[j * HD:(j + 1) * HD, (t - 1) * P:(t + 1) * P], v[:, par, mt, c:c + HD],
                                 probT[:, j, mt, :], start=(mt == 0), stop=(mt == NT - 1), skip_group_check=True)
                ins.then_inc(pv_ps, 1)

            def spread_recip(b, g):
                pe.wait_ge(wide_done, G * b + g + 1)
                for t in range(NT):
                    ins = nc.tensor.transpose(t_bank[0][:, t * P:(t + 1) * P],
                                              recip_wide[:, J * t:J * t + J, :].rearrange("p a d -> p (a d)"),
                                              ident[:, :])
                ins.then_inc(r_ps, 1)

            def prob_transpose(b, s, j):
                pe.wait_ge(exp_done, 64 * b + J * s + j + 1)
                for mt in range(NT):
                    ins = nc.tensor.transpose(t_bank[j % 2][:, mt * P:(mt + 1) * P],
                                              prob[:, s % 2, j, mt * P:(mt + 1) * P], ident[:, :])
                ins.then_inc(p_ps, 1)

            def t_bank_freed(n, b, s):
                if n == 0 or (s - 1) % STEPS in ACT_COPIES_3:
                    need(pe, pT_act, copies_act(b, s))
                else:
                    need(pe, pT_dve, copies_dve(b, s))

            pe.wait_ge(w_lo, 4 * NT)
            for t in range(NT):
                y_rows(0, t, first_y_bank[t], 0)
            pe.wait_ge(outT_sb, NT * B)
            pe.wait_ge(bn_chain, BN_BANK)
            for t in range(2):
                x1_transpose(0, t, first_xT_bank[t])
            for s in range(AHEAD, STEPS):
                kind, i, _ = SLOTS[s]
                if s in (AHEAD + 1, AHEAD + 2):
                    x1_transpose(0, s - AHEAD + 1, first_xT_bank[s - AHEAD + 1])
                if s == AHEAD:
                    pe.wait_ge(y_sum, 1)
                elif s == AHEAD + 1:
                    pe.wait_ge(xT_lo, 1)
                else:
                    pe.wait_ge(freed[SLOTS[s - 2][0]], SLOTS[s - 2][1] + 1)
                dense(kind, 0, i, range(NT), dense_bank[s % 2])
            scores(0, 0, (0, 1, 2))
            scores(0, 0, (3,))

            def batch(b, par, first, last):
                reader = [(freed[SLOTS[s][0]], NT * b + SLOTS[s][1] + 1) for s in (STEPS - 2, STEPS - 1)]
                for s in range(STEPS):
                    kind, i, rel = SLOTS[s]
                    there = is_live(s, first, last)
                    other = (s + 1) % 2
                    group_end = s % NT == 0 and not (first and s == 0)
                    late = s in XT_EARLY

                    def next_scores(heads):
                        if s + 1 < STEPS:
                            scores(b, s + 1, heads)
                        elif not last:
                            scores(b + 1, 0, heads)

                    def dense_half(half):
                        if there:
                            if half == 0:
                                pe.wait_ge(*reader[s % 2])
                            dense(kind, b + rel, i, (2 * half, 2 * half + 1), dense_bank[s % 2])

                    next_scores((0, 1, 2))
                    if s in XT_EARLY and not last:
                        pe.wait_ge(*reader[s % 2])
                        x1_transpose(b + 1, XT_EARLY[s], dense_bank[s % 2])
                        reader[s % 2] = (xT_lo, NT * (b + 1) + XT_EARLY[s] + 1)
                    if not late:
                        dense_half(0)
                    if last and s == STEPS - 1:
                        dense("o", b, 1, range(NT - 1), last_o_bank[1])
                    if group_end:
                        t_bank_freed(0, b, s)
                        spread_recip(b if s else b - 1, s // NT - 1 if s else G - 1)
                    next_scores((3,))
                    if s > 0 and s % 2 == 0:
                        weigh_v(b, s - 1, par)
                    elif s == 0 and not first:
                        weigh_v(b - 1, STEPS - 1, 1 - par)
                    if group_end:
                        pe.wait_ge(r_sb, G * b + s // NT)
                    if not group_end:
                        t_bank_freed(0, b, s)
                    prob_transpose(b, s, 0)
                    t_bank_freed(1, b, s)
                    prob_transpose(b, s, 1)
                    if s in Y_STEPS and not last:
                        pe.wait_ge(*reader[other])
                        y_rows(b + 1, Y_STEPS[s], dense_bank[other], 1 - par)
                        reader[other] = (y_sum, NT * (b + 1) + Y_STEPS[s] + 1)
                    if s in XT_MIDDLE and not last:
                        pe.wait_ge(*reader[other])
                        x1_transpose(b + 1, XT_MIDDLE[s], dense_bank[other])
                        reader[other] = (xT_lo, NT * (b + 1) + XT_MIDDLE[s] + 1)
                    if not late:
                        dense_half(1)
                    if last and s == STEPS - 2:
                        for n in range(2):
                            pe.wait_ge(*reader[n])
                        dense("o", b, 0, range(NT - 1), last_o_bank[0])
                    if last and s == STEPS - 1:
                        pe.wait_ge(s_max, 64 * B)
                        dense("o", b, 2, range(NT - 1), last_o_bank[2])
                    pe.wait_ge(pT_act, copies_act(b, s, 1))
                    prob_transpose(b, s, 2)
                    pe.wait_ge(pT_act, copies_act(b, s, 2))
                    prob_transpose(b, s, 3)
                    if late:
                        dense_half(0)
                        dense_half(1)
                    if there:
                        reader[s % 2] = (freed[kind], NT * (b + rel) + i + 1)

            iterations(pe, batch)
            pe.wait_ge(pT_act, copies_act(B, 0))
            spread_recip(B - 1, G - 1)
            weigh_v(B - 1, STEPS - 1, 1)
            dense("o", B - 1, 3, range(NT - 1), last_o_bank[3])
            for i in range(NT):
                dense("o", B - 1, i, (NT - 1,), last_o_bank[i])

        @block.scalar
        def _(act):
            def copy(dst, src, scale=1.0):
                return nc.scalar.activation(dst, src, ACT.Copy, scale=scale)

            def split_x(b):
                act.wait_ge(x_in, 16 * b + 16)
                need(act, z_ps, NT * b)
                copy(x_part[0][:, :, :], x_raw[:, :, :]).then_inc(x_hi, 1)

            def adjT_high(b):
                need(act, z_ps, NT * b)
                for t in range(NT):
                    act.wait_ge(adjT_ps, NT * b + t + 1)
                    copy(adjT[0][:, t, :], adjT_bank[t][:, :]).then_inc(adjT_hi, 1)

            def pick_expert(b, part):
                if part == 0:
                    wait_apart(act, route, 5 * b + 4)
                    pick_expert.no = act.value_load(index8[0:1, 0:1], min_val=0, max_val=E - 1)
                need(act, outT_ps, NT * b)
                src = f32(w_exp[part][:, bass.ds(pick_expert.no, 1), :, :]).rearrange("p o t n -> p (o t) n")
                copy(w_sel[part][:, :, :], src).then_inc(sel_lo if part else sel_hi, 1)

            def z_high(b, t):
                act.wait_ge(z_ps, NT * b + t + 1)
                need(act, outT_ps, NT * b)
                copy(zT[0][:, t, :], dense0_bank[t % 2][:, :]).then_inc(z_hi, 1)

            def z_and_expert(b):
                z_high(b, 0)
                pick_expert(b, 0)
                z_high(b, 1)
                pick_expert(b, 1)
                z_high(b, 2)
                z_high(b, 3)

            def copy_outT(b, tiles=range(NT)):
                for t in tiles:
                    act.wait_ge(outT_ps, NT * b + t + 1)
                    if t == 0:
                        need(act, outT_spilled, 16 * b)
                        need(act, outT_st, NT * b)
                    copy(outT[:, t, :], dense0_bank[t % 2][:, :]).then_inc(outT_sb, 1)

            def expert_high(e):
                act.wait_ge(experts_in[e], 16)
                copy(w_exp[0][:, e, :, :], raw[e][:, :, :]).then_inc(experts_hi, 1)

            adjT_high(0)
            split_x(0)
            expert_high(0)
            expert_high(1)
            z_high(0, 0)
            expert_high(2)
            z_high(0, 1)
            expert_high(3)
            z_high(0, 2)
            z_high(0, 3)
            act.wait_ge(experts_hi, E)
            pick_expert(0, 0)
            act.wait_ge(experts_lo, E + 1)
            pick_expert(0, 1)
            def batch0(b):
                adjT_high(b + 1)
                split_x(b + 1)
                copy_outT(b)
                z_and_expert(b + 1)

            batch0(0)
            with act.Fori(1, B - 1) as b:
                batch0(b)
            act.wait_ge(sel_hi, B)
            act.wait_ge(sel_lo, B)

            def weight_high(n):
                m, ht = "kqvo"[n // NT], n % NT
                act.wait_ge(w_ps, n + 1)
                copy(wT[m][0][:, ht, :], bank[n % NT][:, :], QSCALE if m == "q" else 1.0).then_inc(w_hi, 1)

            for i in range(NT):
                for n in W_WITH_OUT[i]:
                    weight_high(n)
                copy_outT(B - 1, (i,))
            for tiles in W_LATER:
                for n in tiles:
                    weight_high(n)

            layer0_over(act)

            def relu_yT(b, t, par):
                if t == 0:
                    act.wait_ge(yT_in, 16 * b + 16)
                nc.scalar.activation(v[:, par, t, :], v[:, par, t, :], ACT.Relu,
                                     bias=bn_bias[:, bass.ds(b, 1), t:t + 1].rearrange("p o c -> p (o c)"),
                                     scale=bn_scale[:, bass.ds(b, 1), t:t + 1].rearrange("p o c -> p (o c)")).then_inc(yT_relu, 1)

            def xT_high(b, t, ps):
                act.wait_ge(xT_ps, NT * b + t + 1)
                need(act, dense_ps["q"], NT * b)
                copy(xT[0][:, :, t * P:(t + 1) * P], by_block(ps)).then_inc(xT_hi, 1)

            def dense_out(s, b, par):
                kind, i, _ = SLOTS[s]
                ps = dense_bank[s % 2]
                act.wait_ge(dense_ps[kind], NT * b + i + 1)
                if kind == "v":
                    if i == 0:
                        act.wait_ge(y_ps, NT * b + NT)
                    copy(v[:, par, i, :], ps[:, :]).then_inc(v_done, 1)
                else:
                    need(act, packed[kind], 64 * (NT * b + i))
                    copy(stage[kind][0][:, :], ps[:, :]).then_inc(stage_hi[kind], 1)

            def exp(b, s, j):
                g, t = s // NT, s % NT
                if j == 0:
                    act.wait_ge(neg_done, 16 * b + s + 1)
                    if t == 0:
                        need(act, wide_done, G * b + g - 1)
                nc.scalar.activation(prob[:, s % 2, j, :], prob[:, s % 2, j, :], ACT.Exp, scale=2.0,
                                     bias=neg_max[:, s % 2, j:j + 1],
                                     accum_out=row_sum[:, g % 2, J * t + j:J * t + j + 1]).then_inc(exp_done, 1)

            def copy_probT(b, s, j):
                act.wait_ge(p_ps, 64 * b + J * s + j + 1)
                copy(probT[:, j, :, s % 2 * P:(s % 2 + 1) * P], by_block(t_bank[j % 2])).then_inc(pT_act, 1)

            def copy_recip(b, g):
                act.wait_ge(r_ps, G * b + g + 1)
                need(act, oT_lo, G * b + g)
                copy(recip[:, :], t_bank[0][:, :]).then_inc(r_sb, 1)

            def oT_high(b, g):
                act.wait_ge(o_norm, G * b + g + 1)
                if g == 0:
                    need(act, dense_ps["o"], NT * b)
                copy(oT[0][:, g, :], recip[:, :]).then_inc(oT_hi, 1)

            act.wait_ge(bn_ready, 1)
            for t in range(NT):
                relu_yT(0, t, 0)
            for t in range(NT):
                xT_high(0, t, first_xT_bank[t])
            for s in range(AHEAD, STEPS):
                dense_out(s, 0, 0)
            for j in range(J):
                exp(0, 0, j)

            def batch(b, par, first, last):
                for s in range(STEPS):
                    nb, ns = (b, s + 1) if s + 1 < STEPS else (b + 1, 0)
                    ahead = not (last and ns == 0)
                    group_end = s % NT == 0 and not (first and s == 0)
                    gb, gg = (b, s // NT - 1) if s > 0 else (b - 1, G - 1)
                    if group_end:
                        copy_recip(gb, gg)
                    if s in XT_EARLY and not last:
                        xT_high(b + 1, XT_EARLY[s], xT_bank[XT_EARLY[s]])
                    copy_probT(b, s, 0)
                    copy_probT(b, s, 1)
                    if s in OT_STEPS and not (first and s == 0):
                        oT_high(b if s else b - 1, OT_STEPS[s])
                    if s in XT_MIDDLE and not last:
                        xT_high(b + 1, XT_MIDDLE[s], xT_bank[XT_MIDDLE[s]])
                    if ahead:
                        exp(nb, ns, 0)
                        exp(nb, ns, 1)
                    copy_probT(b, s, 2)
                    if s in ACT_COPIES_3:
                        copy_probT(b, s, 3)
                    kind, i, rel = SLOTS[s]
                    if kind != "o" and is_live(s, first, last):
                        dense_out(s, b + rel, 1 - par)
                    if ahead:
                        exp(nb, ns, 2)
                        exp(nb, ns, 3)
                    if s in RELU_STEPS and not last:
                        for t in RELU_STEPS[s]:
                            relu_yT(b + 1, t, 1 - par)

            iterations(act, batch)
            copy_recip(B - 1, G - 1)
            oT_high(B - 1, G - 1)

        @block.vector
        def _(dve):
            tt = nc.vector.tensor_tensor

            def low(dst, ps, hi):
                return tt(dst, ps, f32(hi), ALU.subtract)

            def sum_x(b):
                dve.wait_ge(x_in, 16 * b + 16)
                tt(x_sum[:, :], x_raw[:, 0, :], x_raw[:, 1, :], ALU.add).then_inc(x_added, 1)
                for t in (2, 3):
                    dve.wait_ge(x_added, 3 * b + t - 1)
                    tt(x_sum[:, :], x_sum[:, :], x_raw[:, t, :], ALU.add).then_inc(x_added, 1)

            def adjT_low(b):
                need(dve, z_ps, NT * b)
                for t in range(NT):
                    dve.wait_ge(adjT_hi, NT * b + t + 1)
                    low(adjT[1][:, t, :], adjT_bank[t][:, :], adjT[0][:, t, :]).then_inc(adjT_lo, 1)

            def score(b):
                need(dve, score_ps, b)
                wait_apart(dve, x_added, 3 * b + 3)
                for e in range(E):
                    wait_apart(dve, scored, E * b + e - 1)
                    nc.vector.tensor_tensor_reduce(x_rw[:, e % 2, :], x_sum[:, :], rw[:, :, e], 1.0, 0.0, ALU.mult, ALU.add,
                                                   score_part[:, e:e + 1]).then_inc(scored, 1)

            def pick(b):
                n = 5 * b
                dve.wait_ge(score_ps, b + 1)
                tt(score8[:, 0:E], score_bank[0:1, 0:E], rb[:, :], ALU.add).then_inc(route, 1)
                wait_apart(dve, route, n + 1)
                nc.vector.max(best8[:, :], score8[:, :]).then_inc(route, 1)
                wait_apart(dve, route, n + 2)
                wait_apart(dve, sel_lo, b)
                nc.vector.max_index(index8[:, :], best8[:, :], score8[:, :]).then_inc(route, 1)
                dve.wait_ge(route, n + 3)
                nc.vector.tensor_copy(indexf[:, :], index8[:, :]).then_inc(route, 1)
                dve.wait_ge(route, n + 4)
                nc.vector.tensor_scalar(onehot_row[:, bass.ds(b, 1), :].rearrange("p o e -> p (o e)"),
                                        expert_no[:, :], indexf[:, 0:1], None, ALU.is_equal).then_inc(route, 1)

            def expert_low(e, tiles):
                dve.wait_ge(experts_hi, e + 1)
                tt(w_exp[1][:, e, tiles, :], raw[e][:, tiles, :], f32(w_exp[0][:, e, tiles, :]),
                   ALU.subtract).then_inc(experts_lo, 1)

            def z_low(b, tiles=range(NT)):
                need(dve, outT_ps, NT * b)
                for t in tiles:
                    dve.wait_ge(z_hi, NT * b + t + 1)
                    low(zT[1][:, t, :], dense0_bank[t % 2][:, :], zT[0][:, t, :]).then_inc(z_lo, 1)

            def out_stats(b, t):
                dve.wait_ge(outT_sb, NT * b + t + 1)
                nc.vector.bn_stats(st_bn[:, t, :], outT[:, t, :]).then_inc(outT_st, 1)
                wait_apart(dve, outT_st, NT * b + t + 1)
                if t == 0:
                    wait_apart(dve, outT_kept, b)
                nc.vector.bn_aggr(mv_now[:, t, :], st_bn[:, t, :]).then_inc(outT_mv, 1)

            def keep_stats(b):
                dve.wait_ge(outT_mv, NT * b + NT)
                nc.vector.tensor_copy(mv[:, bass.ds(b, 1), :].rearrange("p o c -> p (o c)"),
                                      mv_now[:, :, :].rearrange("p t c -> p (t c)")).then_inc(outT_kept, 1)

            dve.wait_ge(consts_made, 5 + E)
            adjT_low(0)
            dve.wait_ge(x_hi, 1)
            tt(x_part[1][:, :, :], x_raw[:, :, :], f32(x_part[0][:, :, :]), ALU.subtract).then_inc(x_lo, 1)
            sum_x(0)
            z_low(0, (0,))
            dve.wait_ge(router_in, 16 * 2)
            score(0)
            z_low(0, (1,))
            pick(0)
            expert_low(2, slice(0, NT))
            z_low(0, (2,))
            expert_low(3, slice(0, NT // 2))
            z_low(0, (3,))
            def batch0(b):
                adjT_low(b + 1)
                sum_x(b + 1)
                out_stats(b, 0)
                score(b + 1)
                out_stats(b, 1)
                out_stats(b, 2)
                pick(b + 1)
                out_stats(b, 3)
                keep_stats(b)
                z_low(b + 1)

            batch0(0)
            with dve.Fori(1, B - 1) as b:
                batch0(b)
            def weight_low(n):
                m, ht = "kqvo"[n // NT], n % NT
                dve.wait_ge(w_hi, n + 1)
                if m == "q":
                    ins = nc.vector.scalar_tensor_tensor(out=wT[m][1][:, ht, :], in0=bank[n % NT][:, :], scalar=QSCALE,
                                                         in1=f32(wT[m][0][:, ht, :]), op0=ALU.mult, op1=ALU.subtract)
                else:
                    ins = low(wT[m][1][:, ht, :], bank[n % NT][:, :], wT[m][0][:, ht, :])
                ins.then_inc(w_lo, 1)

            chain = [0]

            def link(ins):
                chain[0] += 1
                ins.then_inc(bn_chain, 1)
                dve.wait_ge(bn_chain, chain[0])

            dve.wait_ge(onehot_ps, 1)
            link(nc.vector.tensor_copy(onehot[:, :, :].rearrange("p b e -> p (b e)"), onehot_bank[:, 0:B * E]))
            link(nc.vector.tensor_copy(gam_bet[:, :, :, :].rearrange("p n e t -> p (n e t)"),
                                       onehot_bank[:, B * E:B * E + 2 * E * NT]))
            assert chain[0] == BN_BANK
            link(nc.vector.tensor_reduce(inv_cnt[:, :], onehot[:, :, :].rearrange("p b e -> p e b"), AX.X, ALU.add))
            link(nc.vector.tensor_scalar(inv_cnt[:, :], inv_cnt[:, :], 1.0 / N, None, ALU.max))
            link(nc.vector.reciprocal(inv_cnt[:, :], inv_cnt[:, :]))

            for i in range(NT):
                for n in W_WITH_OUT[i]:
                    weight_low(n)
                out_stats(B - 1, i)
            keep_stats(B - 1)

            mean_b = mv[:, :, :].rearrange("p b (t c) -> p b t c", c=2)[:, :, :, 0]
            var_b = mv[:, :, :].rearrange("p b (t c) -> p b t c", c=2)[:, :, :, 1]
            dve.wait_ge(outT_kept, B)
            link(tt(ex2[:, :, :], mean_b, mean_b, ALU.mult))
            link(tt(ex2[:, :, :], ex2[:, :, :], var_b, ALU.add))
            wide = [P, E, NT, B]
            pick_e = onehot[:, :, :].rearrange("p b (e o) -> p e o b", o=1).broadcast_to(wide)
            prod_e = prod[:, :].rearrange("p (e t b) -> p e t b", e=E, t=NT)
            for src, dst in ((mean_b, sum1), (ex2[:, :, :], sum2)):
                link(tt(prod_e, src.rearrange("p b (o t) -> p o t b", o=1).broadcast_to(wide), pick_e, ALU.mult))
                link(nc.vector.tensor_reduce(dst[:, :, :], prod_e, AX.X, ALU.add))
                link(tt(dst[:, :, :], dst[:, :, :],
                        inv_cnt[:, :].rearrange("p (e o) -> p e o", o=1).broadcast_to([P, E, NT]), ALU.mult))
            link(tt(scale_e[:, :, :], sum1[:, :, :], sum1[:, :, :], ALU.mult))
            link(tt(sum2[:, :, :], sum2[:, :, :], scale_e[:, :, :], ALU.subtract))
            link(nc.vector.tensor_scalar(sum2[:, :, :], sum2[:, :, :], EPS, None, ALU.add))
            assert chain[0] == BN_VAR
            for n in W_LATER[0]:
                weight_low(n)
            dve.wait_ge(bn_pow, 1)
            link(tt(scale_e[:, :, :], sum2[:, :, :], gam_bet[:, 0, :, :], ALU.mult))
            link(tt(bias_e[:, :, :], sum1[:, :, :], scale_e[:, :, :], ALU.mult))
            link(tt(bias_e[:, :, :], gam_bet[:, 1, :, :], bias_e[:, :, :], ALU.subtract))
            wide = [P, B, NT, E]
            pick_b = onehot[:, :, :].rearrange("p b (o e) -> p b o e", o=1).broadcast_to(wide)
            prod_b = prod[:, :].rearrange("p (b t e) -> p b t e", b=B, t=NT)
            for src, dst in ((scale_e, bn_scale), (bias_e, bn_bias)):
                link(tt(prod_b, src[:, :, :].rearrange("p e (o t) -> p o t e", o=1).broadcast_to(wide), pick_b, ALU.mult))
                link(nc.vector.tensor_reduce(dst[:, :, :], prod_b, AX.X, ALU.add))
            dve.wait_ge(bn_chain, chain[0])
            nc.vector.memset(veps[:, :, :, :], 1.0).then_inc(bn_ready, 1)
            for n in W_LATER[1]:
                weight_low(n)

            layer0_over(dve)

            def norm_stats(which, b, t, sum_sem, st_sem, mv_sem, rstd_sem):
                dve.wait_ge(sum_sem, NT * b + t + 1)
                nc.vector.bn_stats(st_ln[:, which, t % 2, :], z[:, t, :]).then_inc(st_sem, 1)
                wait_apart(dve, st_sem, NT * b + t + 1)
                nc.vector.bn_aggr(mv_ln[:, which, t % 2, :], st_ln[:, which, t % 2, :]).then_inc(mv_sem, 1)

            def normalise(which, b, t, rstd_sem, done_sem):
                dve.wait_ge(rstd_sem, NT * b + t + 1)
                nc.vector.tensor_scalar(z[:, t, :], z[:, t, :], mv_ln[:, which, t % 2, 0:1],
                                        rstd[:, which, t % 2, 0:1], ALU.subtract, ALU.mult).then_inc(done_sem, 1)

            def add_y(b, t, ps):
                dve.wait_ge(x1_x_in[t], 16 * b + 16)
                dve.wait_ge(y_ps, NT * b + t + 1)
                tt(z[:, t, :], ps[:, :], z[:, t, :], ALU.add).then_inc(y_sum, 1)

            def x1_stats(b, t):
                norm_stats(0, b, t, y_sum, y_st, y_mv, y_rstd)

            def x1_norm(b, t):
                normalise(0, b, t, y_rstd, x1_done)

            def xT_low(b, t, ps):
                dve.wait_ge(xT_hi, NT * b + t + 1)
                low(xT[1][:, :, t * P:(t + 1) * P], by_block(ps),
                    xT[0][:, :, t * P:(t + 1) * P]).then_inc(xT_lo, 1)

            def stage_low(s, b):
                kind, i, _ = SLOTS[s]
                dve.wait_ge(stage_hi[kind], NT * b + i + 1)
                low(stage[kind][1][:, :], dense_bank[s % 2][:, :], stage[kind][0][:, :]).then_inc(stage_lo[kind], 1)

            def bias_and_max(b, s, heads):
                g, t = s // NT, s % NT
                if heads[0] == 0:
                    dve.wait_ge(adj1_in[t], 16 * b + 16)
                    need(dve, p_ps, 64 * b + J * (s - 1))
                    if t == 0:
                        need(dve, live_chain, 3 * (G * b + g - 1))
                for j in heads:
                    wait_apart(dve, s_ps, 64 * b + J * s + j + 1)
                    nc.vector.tensor_tensor_reduce(prob[:, s % 2, j, :], s_bank[j][:, :], adj_sb[:, t, :], 1.0, LOWEST,
                                                   ALU.add, ALU.max,
                                                   row_max[:, g % 2, J * t + j:J * t + j + 1]).then_inc(s_max, 1)

            def negate_max(b, s):
                g, t = s // NT, s % NT
                dve.wait_ge(s_max, 64 * b + J * s + J)
                need(dve, exp_done, 64 * b + J * (s - 1))
                nc.vector.tensor_scalar(neg_max[:, s % 2, :], row_max[:, g % 2, J * t:J * t + J], -2.0, None,
                                        ALU.mult).then_inc(neg_done, 1)

            def copy_probT(b, s, j):
                dve.wait_ge(p_ps, 64 * b + J * s + j + 1)
                nc.vector.tensor_copy(probT[:, j, :, s % 2 * P:(s % 2 + 1) * P],
                                      by_block(t_bank[j % 2])).then_inc(pT_dve, 1)

            def inverse_sum(b, g):
                dve.wait_ge(exp_done, 64 * b + 16 * g + 16)
                need(dve, wide_done, G * b + g)
                nc.vector.reciprocal(inv_sum[:, :], row_sum[:, g % 2, :]).then_inc(inv_half, 1)
                dve.wait_ge(live_chain, 3 * (G * b + g) + 3)
                dve.wait_ge(inv_half, G * b + g + 1)
                nc.vector.tensor_tensor(zeros_inv[:, :], live[:, :], inv_sum[:, :], ALU.mult).then_inc(inv_done, 1)

            def weigh(b, g):
                dve.wait_ge(r_sb, G * b + g + 1)
                dve.wait_ge(pv_ps, 8 * b + 2 * g + 2)
                tt(recip[:, :], pv_bank[:, :], recip[:, :], ALU.mult).then_inc(o_norm, 1)

            def oT_low(b, g):
                dve.wait_ge(oT_hi, G * b + g + 1)
                low(oT[1][:, g, :], recip[:, :], oT[0][:, g, :]).then_inc(oT_lo, 1)

            def add_residual(b, t, ps):
                dve.wait_ge(x1_back, 16 * b + 16)
                dve.wait_ge(dense_ps["o"], NT * b + t + 1)
                tt(z[:, t, :], ps[:, :], z[:, t, :], ALU.add).then_inc(f_sum, 1)

            def out_stats1(b, t):
                norm_stats(1, b, t, f_sum, f_st, f_mv, f_rstd)

            def out_norm(b, t):
                normalise(1, b, t, f_rstd, f_done)

            for t in range(NT):
                add_y(0, t, first_y_bank[t])
                x1_stats(0, t)
                if t > 0:
                    x1_norm(0, t - 1)
                if t > 1:
                    xT_low(0, t - 2, first_xT_bank[t - 2])
            x1_norm(0, NT - 1)
            for t in (NT - 2, NT - 1):
                xT_low(0, t, first_xT_bank[t])
            for s in range(AHEAD, STEPS):
                if SLOTS[s][0] != "v":
                    stage_low(s, 0)
            bias_and_max(0, 0, (0, 1, 2))
            bias_and_max(0, 0, (3,))
            negate_max(0, 0)

            def batch(b, par, first, last):
                for s in range(STEPS):
                    nb, ns = (b, s + 1) if s + 1 < STEPS else (b + 1, 0)
                    ahead = not (last and ns == 0)
                    group_end = s % NT == 0 and not (first and s == 0)
                    gb, gg = (b, s // NT - 1) if s > 0 else (b - 1, G - 1)
                    if s > 0 and s - 1 not in ACT_COPIES_3:
                        copy_probT(b, s - 1, 3)
                    elif s == 0 and not first:
                        copy_probT(b - 1, STEPS - 1, 3)
                    if ahead:
                        bias_and_max(nb, ns, (0, 1, 2))
                    if s > 0:
                        (kind, i, rel), there = SLOTS[s - 1], is_live(s - 1, first, last)
                    else:
                        (kind, i, _), rel, there = SLOTS[STEPS - 1], 0, not first
                    if kind in "kq" and there:
                        stage_low((s - 1) % STEPS, b + rel)
                    if ahead:
                        bias_and_max(nb, ns, (3,))
                        negate_max(nb, ns)
                    if s in XT_EARLY and not last:
                        xT_low(b + 1, XT_EARLY[s], xT_bank[XT_EARLY[s]])
                    if kind == "o" and there:
                        add_residual(b - 1, i, dense_bank[(s - 1) % 2])
                        out_stats1(b - 1, i)
                    if s in O_NORMED and not first:
                        out_norm(b - 1, O_NORMED[s])
                    if s in Y_NORMED and not last:
                        x1_norm(b + 1, Y_NORMED[s])
                    if s % NT == 3:
                        inverse_sum(b, s // NT)
                    if s > 1 and s - 1 in OT_STEPS:
                        oT_low(b, OT_STEPS[s - 1])
                    if group_end:
                        weigh(gb, gg)
                    if s == 0 and not first:
                        oT_low(b - 1, OT_STEPS[s])
                    if s in Y_STEPS and not last:
                        add_y(b + 1, Y_STEPS[s], y_bank[Y_STEPS[s]])
                        x1_stats(b + 1, Y_STEPS[s])
                    if s in XT_MIDDLE and not last:
                        xT_low(b + 1, XT_MIDDLE[s], xT_bank[XT_MIDDLE[s]])

            iterations(dve, batch)
            copy_probT(B - 1, STEPS - 1, 3)
            weigh(B - 1, G - 1)
            oT_low(B - 1, G - 1)
            for t in range(NT):
                add_residual(B - 1, t, last_o_bank[t])
                out_stats1(B - 1, t)
                if t > 0:
                    out_norm(B - 1, t - 1)
            out_norm(B - 1, NT - 1)


BN_VAR = 16
BN_BANK = 2

_INS = ["x", "adj", "L0_gnn_router_w", "L0_gnn_router_b", "L0_gnn_expert_w", "L0_gnn_bn_gamma", "L0_gnn_bn_beta",
        "L1_gnn_Wq", "L1_gnn_Wk", "L1_gnn_Wv", "L1_gnn_Wo"]


def kernel(**inputs):
    import numpy as _np
    import concourse.bacc as _bacc
    from concourse import mybir as _mybir
    from concourse.bass_utils import run_bass_kernel_spmd as _run

    nc = _bacc.Bacc("TRN2", target_bir_lowering=False, num_devices=1)
    arrays, args = {}, []
    for name in _INS:
        a = _np.ascontiguousarray(inputs[name])
        arrays[f"in_{name}_dram"] = a
        args.append(nc.dram_tensor(f"in_{name}_dram", a.shape, _mybir.dt.from_np(a.dtype), kind="ExternalInput").ap())
    args.append(nc.dram_tensor("out_0_dram", (B, N, H), _mybir.dt.from_np(_np.dtype("float32")),
                               kind="ExternalOutput").ap())
    gnn_program(nc, *args)
    r = _run(nc, [arrays], core_ids=[0])
    return r.results[0]["out_0_dram"]
```
